# Optimizing a Trainium2 kernel written in Bass

```python
import numpy as np
import jax
import jax.numpy as jnp

def _softmax(x, axis=-1):
    return jax.nn.softmax(x, axis=axis)

def _gelu(x):
    return jax.nn.gelu(x, approximate=True)

def _silu(x):
    return jax.nn.silu(x)

def _sigmoid(x):
    return jax.nn.sigmoid(x)

def _layernorm(x, axis=-1, eps=1e-05):
    m = jnp.mean(x, axis=axis, keepdims=True)
    v = jnp.var(x, axis=axis, keepdims=True)
    return (x - m) / jnp.sqrt(v + eps)

def _scatter_add(tgt, idx, src, axis=0):
    return tgt.at[idx].add(src)

def _segment_sum(src, seg, n):
    return jax.ops.segment_sum(src, seg, n)
kernel_name = 'mk_adj_resnorm_d2_adj_r2_55b89d'

def setup_inputs(seed: int=0):
    np.random.seed(seed)
    _w = jnp.asarray

    def _rec_inputs():
        import jax
        import jax.numpy as jnp
        _gk = jax.random.key(seed)
        x = -0.0001538 + 1 * jax.random.normal(jax.random.fold_in(_gk, 1), (8, 1024, 384), jnp.float32)
        _w = (1.0 + jnp.arange(1024, dtype=jnp.float32)) ** (-0.5)
        _w = _w / _w.mean()
        _pij = jnp.clip(0.00195312 * _w[:, None] * _w[None, :], 0.0, 1.0)
        _a = jax.random.uniform(jax.random.fold_in(_gk, 2), (8, 1024, 1024)) < _pij
        _a = jnp.logical_or(_a, jnp.swapaxes(_a, -1, -2))
        _a = jnp.logical_or(_a, jnp.eye(1024, dtype=bool))
        _af = _a.astype(jnp.float32)
        _af = _af * jax.random.uniform(jax.random.fold_in(_gk, 3), (8, 1024, 1024), jnp.float32, 0.05, 5.06092)
        adj = _af
        return (x, adj)
    x, adj = _rec_inputs()

    def _L0_gnn_setup():
        import jax, jax.numpy as jnp
        import numpy as np
        D_MODEL = 384
        NHEADS = 8
        D_FF = 1536
        B, N = (8, 512)
        EPS = 1e-06

        def _rmsnorm(x, alpha, gamma):
            x = x * jax.lax.rsqrt(jnp.mean(x * x, axis=-1, keepdims=True) + EPS)
            return alpha * x + gamma
        key = jax.random.key(seed)
        ks = jax.random.split(key, 10)
        d, f = (D_MODEL, D_FF)
        s = 1.0 / np.sqrt(d)
        inp = {'x': jax.random.normal(ks[0], (B, N, d), dtype=jnp.float32), 'attn_bias': jax.random.normal(ks[1], (B, N, N), dtype=jnp.float32), 'wq': jax.random.normal(ks[2], (d, d), dtype=jnp.float32) * s, 'bq': jnp.zeros((d,), jnp.float32), 'wk': jax.random.normal(ks[3], (d, d), dtype=jnp.float32) * s, 'bk': jnp.zeros((d,), jnp.float32), 'wv': jax.random.normal(ks[4], (d, d), dtype=jnp.float32) * s, 'bv': jnp.zeros((d,), jnp.float32), 'wo': jax.random.normal(ks[5], (d, d), dtype=jnp.float32) * s, 'bo': jnp.zeros((d,), jnp.float32), 'w1': jax.random.normal(ks[6], (d, f), dtype=jnp.float32) * s, 'b1': jnp.zeros((f,), jnp.float32), 'w2': jax.random.normal(ks[7], (f, d), dtype=jnp.float32) * (1.0 / np.sqrt(f)), 'b2': jnp.zeros((d,), jnp.float32), 'alpha1': jnp.ones((d,), jnp.float32), 'gamma1': jnp.ones((d,), jnp.float32), 'alpha2': jnp.ones((d,), jnp.float32), 'gamma2': jnp.ones((d,), jnp.float32)}
        return inp
    _L0_gnn_all = _L0_gnn_setup()
    _L0_gnn_in = {k: v for k, v in _L0_gnn_all.items() if k in ('wq', 'bq', 'wk', 'bk', 'wv', 'bv', 'wo', 'bo', 'w1', 'b1', 'w2', 'b2', 'alpha1', 'gamma1', 'alpha2', 'gamma2')}
    del _L0_gnn_all

    def _L1_gnn_setup():
        import jax, jax.numpy as jnp
        import numpy as np
        B, N, D, H = (8, 512, 384, 12)
        HD = D // H

        def _split_heads(x):
            b, n, _ = x.shape
            return x.reshape(b, n, H, HD).transpose(0, 2, 1, 3)
        key = jax.random.key(seed)
        ks = jax.random.split(key, 10)
        input_graph = jax.random.normal(ks[0], (B, N, D), dtype=jnp.float32)
        u = jax.random.uniform(ks[1], (B, N, N), dtype=jnp.float32)
        keep = jax.random.uniform(ks[2], (B, N, N)) < 0.15
        adj = jnp.where(keep, u, 0.0)
        s = 1.0 / np.sqrt(D)
        Wq = jax.random.normal(ks[3], (D, D), dtype=jnp.float32) * s
        bq = jnp.zeros((D,), dtype=jnp.float32)
        Wk = jax.random.normal(ks[4], (D, D), dtype=jnp.float32) * s
        bk = jnp.zeros((D,), dtype=jnp.float32)
        Wv = jax.random.normal(ks[5], (D, D), dtype=jnp.float32) * s
        bv = jnp.zeros((D,), dtype=jnp.float32)
        beta = jnp.asarray(0.1, dtype=jnp.float32)
        return {'input_graph': input_graph, 'adj': adj, 'Wq': Wq, 'bq': bq, 'Wk': Wk, 'bk': bk, 'Wv': Wv, 'bv': bv, 'beta': beta}
    _L1_gnn_all = _L1_gnn_setup()
    _L1_gnn_in = {k: v for k, v in _L1_gnn_all.items() if k in ('Wq', 'bq', 'Wk', 'bk', 'Wv', 'bv', 'beta')}
    del _L1_gnn_all
    return {'x': x, 'adj': adj, 'L0_gnn_wq': _L0_gnn_in['wq'], 'L0_gnn_bq': _L0_gnn_in['bq'], 'L0_gnn_wk': _L0_gnn_in['wk'], 'L0_gnn_bk': _L0_gnn_in['bk'], 'L0_gnn_wv': _L0_gnn_in['wv'], 'L0_gnn_bv': _L0_gnn_in['bv'], 'L0_gnn_wo': _L0_gnn_in['wo'], 'L0_gnn_bo': _L0_gnn_in['bo'], 'L0_gnn_w1': _L0_gnn_in['w1'], 'L0_gnn_b1': _L0_gnn_in['b1'], 'L0_gnn_w2': _L0_gnn_in['w2'], 'L0_gnn_b2': _L0_gnn_in['b2'], 'L0_gnn_alpha1': _L0_gnn_in['alpha1'], 'L0_gnn_gamma1': _L0_gnn_in['gamma1'], 'L0_gnn_alpha2': _L0_gnn_in['alpha2'], 'L0_gnn_gamma2': _L0_gnn_in['gamma2'], 'L1_gnn_Wq': _L1_gnn_in['Wq'], 'L1_gnn_bq': _L1_gnn_in['bq'], 'L1_gnn_Wk': _L1_gnn_in['Wk'], 'L1_gnn_bk': _L1_gnn_in['bk'], 'L1_gnn_Wv': _L1_gnn_in['Wv'], 'L1_gnn_bv': _L1_gnn_in['bv'], 'L1_gnn_beta': _L1_gnn_in['beta']}

def reference(x, adj, L0_gnn_wq, L0_gnn_bq, L0_gnn_wk, L0_gnn_bk, L0_gnn_wv, L0_gnn_bv, L0_gnn_wo, L0_gnn_bo, L0_gnn_w1, L0_gnn_b1, L0_gnn_w2, L0_gnn_b2, L0_gnn_alpha1, L0_gnn_gamma1, L0_gnn_alpha2, L0_gnn_gamma2, L1_gnn_Wq, L1_gnn_bq, L1_gnn_Wk, L1_gnn_bk, L1_gnn_Wv, L1_gnn_bv, L1_gnn_beta):
    import jax
    import jax.numpy as jnp

    def _L0_gnn_ref(x, attn_bias, wq, bq, wk, bk, wv, bv, wo, bo, w1, b1, w2, b2, alpha1, gamma1, alpha2, gamma2):
        import jax, jax.numpy as jnp
        import numpy as np
        D_MODEL = 384
        NHEADS = 8
        D_FF = 1536
        B, N = (8, 512)
        EPS = 1e-06

        def _rmsnorm(x, alpha, gamma):
            x = x * jax.lax.rsqrt(jnp.mean(x * x, axis=-1, keepdims=True) + EPS)
            return alpha * x + gamma
        b, n, d = x.shape
        h = NHEADS
        dh = d // h
        scaling = dh ** (-0.5)

        def split_heads(t):
            return t.reshape(b, n, h, dh).transpose(0, 2, 1, 3)
        q = split_heads(x @ wq + bq)
        k = split_heads(x @ wk + bk)
        v = split_heads(x @ wv + bv)
        scores = jnp.einsum('bhqd,bhkd->bhqk', q, k) * scaling
        scores = scores + attn_bias[:, None, :, :]
        attn = jax.nn.softmax(scores, axis=-1)
        ctx = jnp.einsum('bhij,bhjd->bhid', attn, v)
        ctx = ctx.transpose(0, 2, 1, 3).reshape(b, n, d)
        attn_out = ctx @ wo + bo
        x = _rmsnorm(x + attn_out, alpha1, gamma1)
        ff = jax.nn.silu(x @ w1 + b1) @ w2 + b2
        x = _rmsnorm(x + ff, alpha2, gamma2)
        return x

    def _L1_gnn_ref(input_graph, adj, Wq, bq, Wk, bk, Wv, bv, beta):
        import jax, jax.numpy as jnp
        import numpy as np
        B, N, D, H = (8, 512, 384, 12)
        HD = D // H

        def _split_heads(x):
            b, n, _ = x.shape
            return x.reshape(b, n, H, HD).transpose(0, 2, 1, 3)
        q = _split_heads(input_graph @ Wq + bq)
        k = _split_heads(input_graph @ Wk + bk)
        v = _split_heads(input_graph @ Wv + bv)
        scores = jnp.einsum('bhqd,bhkd->bhqk', q, k) / jnp.sqrt(jnp.asarray(HD, input_graph.dtype))
        adj_e = adj[:, None, :, :]
        scores = scores + beta * adj_e
        scores = jnp.where(adj_e > 0, scores, jnp.asarray(-9000000000000000.0, scores.dtype))
        probs = jax.nn.softmax(scores, axis=-1)
        out = jnp.einsum('bhqk,bhkd->bhqd', probs, v)
        return out.transpose(0, 2, 1, 3).reshape(input_graph.shape[0], input_graph.shape[1], D)
    x = _layernorm(x + _L0_gnn_ref(x, adj, L0_gnn_wq, L0_gnn_bq, L0_gnn_wk, L0_gnn_bk, L0_gnn_wv, L0_gnn_bv, L0_gnn_wo, L0_gnn_bo, L0_gnn_w1, L0_gnn_b1, L0_gnn_w2, L0_gnn_b2, L0_gnn_alpha1, L0_gnn_gamma1, L0_gnn_alpha2, L0_gnn_gamma2), axis=-1)
    x = _layernorm(x + _L1_gnn_ref(x, adj, L1_gnn_Wq, L1_gnn_bq, L1_gnn_Wk, L1_gnn_bk, L1_gnn_Wv, L1_gnn_bv, L1_gnn_beta), axis=-1)
    return x

_drawn_inputs = setup_inputs


def setup_inputs(seed=0):
    import zlib

    import numpy as np

    out = dict(_drawn_inputs(seed))
    spreads = {'L0_gnn_bq': (0.0, 0.8),
     'L0_gnn_bk': (0.0, 0.8),
     'L0_gnn_bv': (0.0, 0.1),
     'L0_gnn_bo': (0.0, 0.1),
     'L0_gnn_b1': (0.0, 0.29),
     'L0_gnn_b2': (0.0, 0.1),
     'L0_gnn_alpha1': (1.0, 0.2),
     'L0_gnn_gamma1': (1.0, 0.2),
     'L0_gnn_alpha2': (1.0, 0.2),
     'L0_gnn_gamma2': (1.0, 0.2),
     'L1_gnn_bq': (0.0, 0.287),
     'L1_gnn_bk': (0.0, 0.8),
     'L1_gnn_bv': (0.0, 0.1)}
    factors = {}
    for name, (base, spread) in spreads.items():
        noise = np.random.default_rng([zlib.crc32(name.encode()), seed]).standard_normal(out[name].shape)
        drawn = base * np.exp(spread * noise) if base else spread * noise
        out[name] = jnp.asarray(drawn.astype(out[name].dtype))
    for name, factor in factors.items():
        out[name] = (out[name] * factor).astype(out[name].dtype)
    return out
```

```python
from contextlib import ExitStack

import concourse.bass as bass
from concourse import mybir

F32 = mybir.dt.float32
F32R = mybir.dt.float32r
ALU = mybir.AluOpType
ACT = mybir.ActivationFunctionType

P = 128
B, N, D = 8, 1024, 384
FF = 1536
QT = N // P
KT = D // P
CH = 512
NC = N // CH
TPC = CH // P
FT = FF // P
HEADS = (8, 12)
HD = (D // HEADS[0], D // HEADS[1])
GROUP = (2, 4)
VCOL = (64, 32)
RMS_EPS, LN_EPS = 1e-6, 1e-5
MASKED = -9e15
BIG = 3.0e38

STEPS = [QT * h for h in HEADS]
STEP0 = [0, STEPS[0]]
NSTEP = sum(STEPS)
GROUPS = [STEPS[l] // GROUP[l] for l in (0, 1)]
GROUP0 = [0, GROUPS[0]]
NGROUP = sum(GROUPS)
XT_UNITS, QK_UNITS, V_UNITS = KT * NC, KT * 2 * NC, QT
PROJ = XT_UNITS + QK_UNITS + V_UNITS
SPLIT = XT_UNITS + QK_UNITS
TR = 2 * NC * KT
HU = NC * FT
ROOTS = 4 * QT
LN_LAG = 6


def head_pieces(layer, m):
    hd, out, d = HD[layer], [], m * P
    while d < (m + 1) * P:
        n = min(hd - d % hd, (m + 1) * P - d)
        out.append((d - m * P, d // hd, d % hd, n))
        d += n
    return out


def stack_copies(layer, is_k):
    if layer == 0:
        return [(0, 1, 0), (0, 1, 48), (1, 2, 0), (1, 2, 48)] if is_k else [(0, 0, 0), (1, 0, 48)]
    return [(0, 1, 0), (0, 1, 32), (1, 1, 64)] if is_k else [(0, 0, 0), (1, 0, 32), (0, 0, 64)]


def stack_dmas(layer, m, is_k):
    return len(head_pieces(layer, m)) * len(stack_copies(layer, is_k))


def staged(layer, m, is_k):
    n = sum(stack_dmas(0, i, is_k) for i in range(KT)) if layer else 0
    return n + sum(stack_dmas(layer, i, is_k) for i in range(m + 1))


def gnn_kernel(nc, x, adj, wq0, bq0, wk0, bk0, wv0, bv0, wo, bo, w1, b1, w2, b2, al1, ga1, al2, ga2,
               wq1, bq1, wk1, bk1, wv1, bv1, beta, out):
    with ExitStack() as ctx:
        def sb(name, shape, dt=F32, at=ctx):
            return at.enter_context(nc.sbuf_tensor(name, shape, dt))

        def sem(name):
            return ctx.enter_context(nc.semaphore(name))

        def dram(name, shape):
            return nc.dram_tensor(name, shape, F32, kind="Internal").ap()

        d_qk = dram("split_qk", [2, KT, 2, P, 2 * KT * P])
        d_v = dram("split_v", [2, P, 2 * KT * D])
        d_o = dram("split_o", [P, 2 * KT * D])
        d_ff = dram("split_ff", [FT, P, 2 * 2 * KT * P])

        X = sb("X", [P, QT, D])
        O = sb("O", [P, QT, D])
        V = sb("V", [P, QT, D])
        bvb = sb("bvb", [P, 2, D])
        rowsc = sb("rowsc", [P, 6, D])
        bo_b, b2_b, al1_b, ga1_b, al2_b, ga2_b = (rowsc[:, i, :] for i in range(6))
        small = sb("small", [P, 4 * KT + FT + 4])
        bqk = small[:, 0:4 * KT].rearrange("p (l w m) -> p l w m", l=2, w=2)
        b1c = small[:, 4 * KT:4 * KT + FT]
        betac, powc, epsr, epsl = (small[:, 4 * KT + FT + i:4 * KT + FT + i + 1] for i in range(4))
        ident = sb("ident", [P, P])
        nmax = sb("nmax", [P, QT, HEADS[1]])
        rsum = sb("rsum", [P, QT, HEADS[1]])
        OT = sb("OT", [P, 2, P])
        stat = sb("stat", [P, QT, 13])
        arena = sb("arena", [P, 24 * N], F32R)

        setup = ExitStack()
        raw = sb("raw", [P, 3, KT * D], at=setup)
        setup.close()
        proj = ExitStack()
        stg = sb("stg", [P, 2, 2, N], F32R, proj)
        xT = sb("xT", [P, 2, KT, N], F32R, proj)
        wqk = sb("wqk", [P, 4, 2 * KT * P], F32R, proj)
        wv = sb("wv", [P, 2, KT, D], F32R, proj)
        proj.close()
        attn = ExitStack()
        A = sb("A", [P, 3, N], at=attn)
        maskt = sb("maskt", [P, N], at=attn)
        PT = sb("PT", [P, 8, QT, P], at=attn)
        T = sb("T", [P, 3, N], at=attn)
        attn.close()
        ffn = ExitStack()
        hT = sb("hT", [P, 2, 2, CH], F32R, ffn)
        hs = sb("hs", [P, 2, CH], at=ffn)
        sq = sb("sq", [P, D], at=ffn)
        x1T = sb("x1T", [P, NC, 2, KT, CH], F32R, ffn)
        oT = sb("oT", [P, 2, KT, CH], F32R, ffn)
        wos = sb("wos", [P, 2, KT, D], F32R, ffn)
        ffn.close()

        ps = ctx.enter_context(nc.psum_tensor("ps", [P, 8, CH], F32))

        def f32(ap):
            return ap.bitcast(F32)

        consts_in = sem("consts_in")
        bias_in = sem("bias_in")
        ident_zero = sem("ident_zero")
        consts_ready = sem("consts_ready")
        pconst_ready = sem("pconst_ready")
        raw_in = [sem(f"raw_in{i}") for i in range(3)]
        w_scaled = sem("w_scaled")
        w_hi = sem("w_hi")
        w_lo = sem("w_lo")
        split_out = [sem(f"split_out{i}") for i in range(3)]
        x_in = [sem(f"x_in{t}") for t in range(QT)]
        wqk_in = [sem(f"wqk_in{i}") for i in range(4)]
        wv_in = sem("wv_in")
        proj_ready = sem("proj_ready")
        proj_hi = sem("proj_hi")
        proj_done = sem("proj_done")
        stg_out = [sem("stg_out_q"), sem("stg_out_k")]
        adj_in = [sem(f"adj_in{i}") for i in range(3)]
        mask_step = sem("mask_step")
        mask_ready = sem("mask_ready")
        scores_ready = sem("scores_ready")
        sum_ready = sem("sum_ready")
        exp_ready = sem("exp_ready")
        pt_ready = sem("pt_ready")
        pt_evacA = sem("pt_evacA")
        pt_evacB = sem("pt_evacB")
        pv_ready = sem("pv_ready")
        ot_evac = sem("ot_evac")
        ob_ready = sem("ob_ready")
        recip_ready = sem("recip_ready")
        norm_done = sem("norm_done")
        wo_in = sem("wo_in")
        ff_in = [sem(f"ff_in{f}") for f in range(FT)]
        tr_ready = sem("tr_ready")
        tr_hi = sem("tr_hi")
        tr_lo = sem("tr_lo")
        ao_ready = sem("ao_ready")
        ao_read = sem("ao_read")
        res_ready = sem("res_ready")
        sq_ready = sem("sq_ready")
        x1_ready = sem("x1_ready")
        dve_step = sem("dve_step")
        rms_ready = sem("rms_ready")
        stats_step = sem("stats_step")
        waits_passed = sem("waits_passed")
        var_ready = sem("var_ready")
        ln_ready = sem("ln_ready")
        root_step = sem("root_step")
        pool_step = sem("pool_step")
        pre2_ready = sem("pre2_ready")
        h_ready = sem("h_ready")
        silu_ready = sem("silu_ready")
        h_hi = sem("h_hi")
        h_lo = sem("h_lo")
        y_step = sem("y_step")
        y_read = sem("y_read")
        x_ready = sem("x_ready")
        r1_ready = sem("r1_ready")
        x_free = sem("x_free")
        out_ready = sem("out_ready")
        out_done = [sem(f"out_done{t}") for t in range(QT)]

        def rows(w):
            return w.rearrange("(k p) n -> p k n", p=P)

        PIECES = []
        for l, (wq_, wk_, wv_) in enumerate(((wq0, wk0, wv0), (wq1, wk1, wv1))):
            PIECES.append((rows(wq_), float(HD[l]) ** -0.5, [d_qk[l, m, 0] for m in range(KT)], "cols"))
            PIECES.append((rows(wk_), None, [d_qk[l, m, 1] for m in range(KT)], "cols"))
            PIECES.append((rows(wv_), None, [d_v[l]], "rows"))
        PIECES.append((rows(wo), None, [d_o], "rows"))
        half = 2 * KT * P
        for i in range(FT // KT):
            fs = range(i * KT, (i + 1) * KT)
            PIECES.append((rows(w1)[:, :, i * D:(i + 1) * D], None, [d_ff[f][:, 0:half] for f in fs], "cols"))
            PIECES.append((rows(w2)[:, i * KT:(i + 1) * KT, :], None, [d_ff[f][:, half:2 * half] for f in fs], "tiles"))
        NP_ = len(PIECES)
        PW = 2 * KT * D

        def split_view(i, part):
            s = arena[:, (i % 3) * PW:(i % 3 + 1) * PW]
            kind = PIECES[i][3]
            if kind == "cols":
                return s.rearrange("p (m h k c) -> p h k m c", m=KT, h=2, k=KT)[:, part]
            if kind == "rows":
                return s.rearrange("p (h k n) -> p h k n", h=2, k=KT)[:, part]
            return s.rearrange("p (f h n) -> p h f n", f=KT, h=2)[:, part]

        def raw_view(i):
            v = raw[:, i % 3, :]
            if PIECES[i][3] == "cols":
                return v.rearrange("p (k m c) -> p k m c", k=KT, m=KT)
            return v.rearrange("p (k n) -> p k n", k=KT)

        def piece_outs(i):
            return len(PIECES[i][2])

        def outs_before(i):
            return sum(piece_outs(j) for j in range(i % 3, i + 1, 3))

        def stack(layer, block, h):
            c = (block * HEADS[layer] + h) * N
            return arena[0:96, c:c + N]

        def v_cols(layer, h):
            return slice(h * HD[layer], (h + 1) * HD[layer])

        def last_of_group(layer, s):
            return s < STEPS[layer] and s % GROUP[layer] == GROUP[layer] - 1

        def wait_alone(eng, sem_, value):
            eng.wait_ge(sem_, value)
            eng.sem_inc(waits_passed, 1)

        def first_weights(sp, l):
            for u in range(4):
                sp.dma_start(f32(wqk[:, u, :]), d_qk[l, u // 2, u % 2]).then_inc(wqk_in[u], 16)
            sp.dma_start(f32(wv[:]).rearrange("p h k n -> p (h k n)"), d_v[l]).then_inc(wv_in, 16)

        def store_and_next(sp, b, t):
            sp.wait_ge(out_ready, b * QT + t + 1)
            sp.dma_start(out[b, t * P:(t + 1) * P, :], O[:, t, :]).then_inc(out_done[t], 16)
            sp.wait_ge(x_free, b * QT + t + 1)
            nb = (b + 1) % B
            sp.dma_start(X[:, t, :], x[nb, t * P:(t + 1) * P, :]).then_inc(x_in[t], 16)

        def rms(link, b, idx, t, gain):
            nc.vector.wait_ge(rms_ready, b * 2 * QT + idx + 1)
            link(nc.vector.scalar_tensor_tensor(out=O[:, t, :], in0=O[:, t, :], scalar=stat[:, t, 2:3], in1=gain,
                                                op0=ALU.mult, op1=ALU.mult))

        def layer_stats(b, src, idx, t):
            nc.vector.bn_stats(stat[:, t, 4:10], src).then_inc(stats_step, 1)
            wait_alone(nc.vector, stats_step, b * 2 * QT + idx + 1)
            nc.vector.bn_aggr(stat[:, t, 10:12], stat[:, t, 4:10]).then_inc(var_ready, 1)

        def layer_norm(b, src, dst, idx, t):
            nc.vector.wait_ge(ln_ready, b * 2 * QT + idx + 1)
            return nc.vector.tensor_scalar(dst, src, stat[:, t, 10:11], stat[:, t, 12:13], ALU.subtract, ALU.mult)

        def inverse_root(pool, b, n, src, eps, dst):
            nc.gpsimd.tensor_tensor(src, src, eps, ALU.add).then_inc(root_step, 1)
            pool.wait_ge(root_step, b * ROOTS + n)
            return nc.gpsimd.tensor_tensor(dst, src, powc, ALU.pow)

        def feed_forward(b, link):
            dve = nc.vector

            def lo_tr(k, hi, lo):
                dve.wait_ge(tr_hi, b * TR + k + 1)
                dve.tensor_tensor(lo, ps[:, 4 + k % 2, :], f32(hi), ALU.subtract).then_inc(tr_lo, 1)

            for c in range(NC):
                for k in range(KT):
                    lo_tr(c * KT + k, oT[:, 0, k, :], oT[:, 1, k, :])
                for j in range(TPC):
                    t = c * TPC + j
                    dve.wait_ge(ao_ready, b * QT + t + 1)
                    dve.tensor_tensor(O[:, t, :], ps[:, 6 + t % 2, 0:D], X[:, t, :], ALU.add).then_inc(ao_read, 1)
                    dve.wait_ge(ao_read, b * QT + t + 1)
                    dve.tensor_tensor(O[:, t, :], O[:, t, :], bo_b, ALU.add).then_inc(res_ready, 1)
                for j in range(TPC):
                    t = c * TPC + j
                    rms(link, b, t, t, al1_b)
                    dve.tensor_tensor(O[:, t, :], O[:, t, :], ga1_b, ALU.add).then_inc(x1_ready, 1)
            for c in range(NC):
                for k in range(KT):
                    lo_tr(NC * KT + c * KT + k, x1T[:, c, 0, k, :], x1T[:, c, 1, k, :])

            def tail_sum(t):
                dve.wait_ge(pre2_ready, b * QT + t + 1)
                dve.wait_ge(y_step, b * HU + (t // TPC + 1) * FT)
                dve.tensor_tensor(O[:, t, :], ps[:, t % TPC, 0:D], O[:, t, :], ALU.add).then_inc(res_ready, 1)

            def tail_norms(t):
                rms(link, b, QT + t, t, al2_b)
                dve.wait_ge(pool_step, b * QT + t + 1)
                link(dve.tensor_tensor(O[:, t, :], O[:, t, :], X[:, t, :], ALU.add))
                layer_stats(b, O[:, t, :], t, t)

            def tail_end(t):
                layer_norm(b, O[:, t, :], X[:, t, :], t, t).then_inc(x_ready, 1)

            for k in range(HU):
                dve.wait_ge(silu_ready, b * HU + k + 1)
                dve.wait_ge(h_hi, b * HU + k + 1)
                dve.tensor_tensor(hT[:, k % 2, 1, :], hs[:, k % 2, :], f32(hT[:, k % 2, 0, :]), ALU.subtract
                                  ).then_inc(h_lo, 1)
                if k == FT:
                    for t in range(TPC):
                        tail_sum(t)
                if k >= FT + 3 and k - FT - 3 < TPC:
                    tail_norms(k - FT - 3)
                if k >= FT + 7 and k - FT - 7 < TPC:
                    tail_end(k - FT - 7)
            for t in range(TPC, QT):
                tail_sum(t)
            for t in range(TPC, QT):
                tail_norms(t)
            for t in range(TPC, QT):
                tail_end(t)

        def out_stats(b, link, t):
            dve = nc.vector
            dve.wait_ge(norm_done, b * NGROUP + GROUP0[1] + (t + 1) * (HEADS[1] // GROUP[1]))
            dve.tensor_tensor(O[:, t, :], O[:, t, :], X[:, t, :], ALU.add).then_inc(x_free, 1)
            dve.wait_ge(x_free, b * QT + t + 1)
            layer_stats(b, O[:, t, :], QT + t, t)

        def transposed_unit(pe, b, k, c, kt):
            if k >= 2:
                pe.wait_ge(tr_lo, b * TR + k - 1)
            for j in range(TPC):
                mm = pe.transpose(ps[:, 4 + k % 2, j * P:(j + 1) * P], O[:, c * TPC + j, kt * P:(kt + 1) * P], ident[:])
            mm.then_inc(tr_ready, 1)

        block = ctx.enter_context(nc.Block())

        @block.sync
        def _(sp):
            for i in range(NP_ + 2):
                if i < NP_:
                    if i >= 3:
                        sp.wait_ge(w_lo, i - 2)
                    sp.dma_start(raw[:, i % 3, :].rearrange("p (k n) -> p k n", k=KT), PIECES[i][0]).then_inc(raw_in[i % 3], 16)
                j = i - 2
                if j >= 0:
                    sp.wait_ge(w_lo, j + 1)
                    s = arena[:, (j % 3) * PW:(j % 3 + 1) * PW].rearrange("p (d n) -> p d n", d=piece_outs(j))
                    for d, dst in enumerate(PIECES[j][2]):
                        sp.dma_start(dst, f32(s[:, d, :])).then_inc(split_out[j % 3], 16)
            for q in range(3):
                sp.wait_ge(split_out[q], 16 * sum(piece_outs(j) for j in range(q, NP_, 3)))
            for t in range(QT):
                sp.dma_start(X[:, t, :], x[0, t * P:(t + 1) * P, :]).then_inc(x_in[t], 16)

            first_weights(sp, 0)

            with sp.Fori(0, B) as b:
                for l in (0, 1):
                    def load_qk(u):
                        m, is_k = u // 2, u % 2
                        sp.wait_ge(proj_ready, b * 2 * PROJ + l * PROJ + XT_UNITS + NC * (u - 3))
                        sp.dma_start(f32(wqk[:, u % 4, :]), d_qk[l, m, is_k]).then_inc(wqk_in[u % 4], 16)

                    def copy_stacks(u):
                        m, is_k = u // 2, u % 2
                        sp.wait_ge(proj_done, b * 2 * PROJ + l * PROJ + XT_UNITS + NC * (u + 1))
                        for row, h, off, n in head_pieces(l, m):
                            for part, blk, at in stack_copies(l, is_k):
                                dst = arena[at + off:at + off + n, (blk * HEADS[l] + h) * N:(blk * HEADS[l] + h + 1) * N]
                                sp.dma_start(f32(dst), f32(stg[row:row + n, is_k, part, :])).then_inc(stg_out[is_k], 16)

                    if l == 1:
                        sp.wait_ge(ao_ready, b * QT + QT)
                        first_weights(sp, l)
                    for u in range(6):
                        copy_stacks(u)
                        if u + 4 < 6:
                            load_qk(u + 4)
                    for q in range(2):
                        wait_alone(sp, stg_out[q], b * 16 * staged(1, KT - 1, q) + 16 * staged(l, KT - 1, q))

                    for t in range(QT):
                        if t >= 3:
                            sp.wait_ge(sum_ready, b * NSTEP + STEP0[l] + (t - 2) * HEADS[l])
                        sp.dma_start(A[:, t % 3, :], adj[b, t * P:(t + 1) * P, :]).then_inc(adj_in[t % 3], 16)
                        if l == 1 and t >= 3:
                            store_and_next(sp, b, t - 3)
                    if l == 0:
                        sp.wait_ge(scores_ready, b * NSTEP + STEPS[0])
                        for f in range(FT):
                            if f == 1:
                                wait_alone(sp, pt_ready, b * 2 * NSTEP + 2 * STEPS[0])
                                sp.wait_ge(pv_ready, b * NGROUP + GROUPS[0])
                                sp.dma_start(f32(wos[:]).rearrange("p h k n -> p (h k n)"), d_o).then_inc(wo_in, 16)
                            w = 2 * half
                            sp.dma_start(f32(arena[:, f * w:(f + 1) * w]), d_ff[f]).then_inc(ff_in[f], 16)
                    else:
                        wait_alone(sp, pt_ready, b * 2 * NSTEP + 2 * NSTEP)
                        sp.wait_ge(pv_ready, b * NGROUP + NGROUP)
                        first_weights(sp, 0)
                        for t in range(QT - 3, QT):
                            store_and_next(sp, b, t)
                        for t in range(QT):
                            wait_alone(sp, out_done[t], b * 16 + 16)
            for i in range(4):
                sp.wait_ge(wqk_in[i], 16 * (2 * B * (2 if i < 2 else 1) + 1))
            sp.wait_ge(wv_in, 16 * (2 * B + 1))
            for t in range(QT):
                sp.wait_ge(x_in[t], 16 * (B + 1))

        @block.gpsimd
        def _(pool):
            nc.gpsimd.memset(ident[:], 0.0).then_inc(ident_zero, 1)
            pool.wait_ge(ident_zero, 1)
            nc.gpsimd.affine_select(out=ident[:], in_=ident[:], compare_op=ALU.not_equal, fill=1.0, base=0,
                                    pattern=[[-1, P]], channel_multiplier=1).then_inc(consts_ready, 1)
            nc.gpsimd.memset(powc, -0.5).then_inc(pconst_ready, 1)
            nc.gpsimd.memset(epsr, RMS_EPS).then_inc(pconst_ready, 1)
            nc.gpsimd.memset(epsl, LN_EPS).then_inc(pconst_ready, 1)
            for i, r in enumerate((bo, b2, al1, ga1, al2, ga2)):
                pool.dma_start(rowsc[:, i, :], r.partition_broadcast(P)).then_inc(consts_in, 16)
            for i, r in enumerate((bv0, bv1)):
                pool.dma_start(bvb[:, i, :], r.partition_broadcast(P)).then_inc(consts_in, 16)
            for i, r in enumerate((bq0, bk0, bq1, bk1)):
                pool.dma_start(bqk[:, i // 2, i % 2, :], r.rearrange("(m p) -> p m", p=P),
                               allow_slow_non_contiguous=True).then_inc(bias_in, 16)
            pool.dma_start(b1c, b1.rearrange("(m p) -> p m", p=P), allow_slow_non_contiguous=True).then_inc(bias_in, 16)
            pool.dma_start(betac, beta.partition_broadcast(P)).then_inc(bias_in, 16)
            pool.wait_ge(consts_in, 16 * 8)
            pool.wait_ge(bias_in, 16 * 6)
            pool.wait_ge(pconst_ready, 3)

            with pool.Fori(0, B) as b:
                for t in range(QT):
                    pool.wait_ge(sq_ready, b * 2 * QT + t + 1)
                    inverse_root(pool, b, t + 1, stat[:, t, 0:1], epsr, stat[:, t, 2:3]).then_inc(rms_ready, 1)
                for t in range(QT):
                    pool.wait_ge(x1_ready, b * QT + t + 1)
                    nc.gpsimd.tensor_tensor(X[:, t, :], X[:, t, :], ga2_b, ALU.add).then_inc(pool_step, 1)
                for t in range(QT):
                    pool.wait_ge(tr_ready, b * TR + NC * KT + (t // TPC + 1) * KT)
                    nc.gpsimd.tensor_tensor(O[:, t, :], O[:, t, :], b2_b, ALU.add).then_inc(pre2_ready, 1)
                n = QT
                for c in range(NC):
                    for t in range(c * TPC, (c + 1) * TPC):
                        n += 1
                        pool.wait_ge(sq_ready, b * 2 * QT + QT + t + 1)
                        inverse_root(pool, b, n, stat[:, t, 0:1], epsr, stat[:, t, 2:3]).then_inc(rms_ready, 1)
                    for t in range(c * TPC, (c + 1) * TPC):
                        n += 1
                        pool.wait_ge(var_ready, b * 2 * QT + t + 1)
                        inverse_root(pool, b, n, stat[:, t, 11:12], epsl, stat[:, t, 12:13]).then_inc(ln_ready, 1)
                for t in range(QT + 3):
                    if t >= 3:
                        pool.wait_ge(var_ready, b * 2 * QT + QT + t - 2)
                        inverse_root(pool, b, 3 * QT + t - 2, stat[:, t - 3, 11:12], epsl,
                                     stat[:, t - 3, 12:13]).then_inc(ln_ready, 1)
                    if t >= QT:
                        continue
                    n = t // 3
                    per = [(QT + 2 - i) // 3 for i in range(3)]
                    if t == 0:
                        pool.wait_ge(stg_out[1], b * 16 * staged(1, KT - 1, 1) + 16 * staged(1, KT - 1, 1))
                    else:
                        pool.wait_ge(mask_ready, b * QT + t)
                    wait_alone(pool, adj_in[t % 3], b * 32 * per[t % 3] + 16 * (per[t % 3] + n + 1))
                    nc.gpsimd.tensor_scalar(maskt[:], A[:, t % 3, :], 0.0, MASKED, ALU.is_le, ALU.mult).then_inc(mask_step, 1)
                    wait_alone(pool, mask_step, b * 2 * QT + 2 * t + 1)
                    nc.gpsimd.tensor_scalar(A[:, t % 3, :], A[:, t % 3, :], betac[:, 0:1], None, ALU.mult).then_inc(mask_step, 1)
                    pool.wait_ge(mask_step, b * 2 * QT + 2 * t + 2)
                    nc.gpsimd.tensor_tensor(A[:, t % 3, :], A[:, t % 3, :], maskt[:], ALU.add).then_inc(mask_ready, 1)

        @block.scalar
        def _(act):
            act.wait_ge(bias_in, 16 * 6)
            for l in (0, 1):
                nc.scalar.mul(bqk[:, l, 0, :], bqk[:, l, 0, :], float(HD[l]) ** -0.5).then_inc(w_scaled, 1)
            scaled = 2
            for i in range(NP_):
                act.wait_ge(raw_in[i % 3], 16 * (i // 3 + 1))
                if PIECES[i][1] is not None:
                    nc.scalar.mul(raw[:, i % 3, :], raw[:, i % 3, :], PIECES[i][1]).then_inc(w_scaled, 1)
                    scaled += 1
                    act.wait_ge(w_scaled, scaled)
                if i >= 3:
                    act.wait_ge(split_out[i % 3], 16 * outs_before(i - 3))
                nc.scalar.copy(split_view(i, 0), raw_view(i)).then_inc(w_hi, 1)

            with act.Fori(0, B) as b:
                for l in (0, 1):
                    for u in range(SPLIT):
                        g = l * PROJ + u
                        act.wait_ge(proj_ready, b * 2 * PROJ + g + 1)
                        src = ps[:, g % 8, :]
                        if u < XT_UNITS:
                            k, c = u // NC, u % NC
                            nc.scalar.copy(xT[:, 0, k, c * CH:(c + 1) * CH], src).then_inc(proj_hi, 1)
                        else:
                            v = u - XT_UNITS
                            m, is_k, c = v // (2 * NC), v // NC % 2, v % NC
                            if c == 0 and m > 0:
                                act.wait_ge(stg_out[is_k], b * 16 * staged(1, KT - 1, is_k) + 16 * staged(l, m - 1, is_k))
                            nc.scalar.activation(stg[:, is_k, 0, c * CH:(c + 1) * CH], src, ACT.Identity,
                                                 bias=bqk[:, l, is_k, m:m + 1]).then_inc(proj_hi, 1)

                    n = STEPS[l]
                    for i in range(-2, n + 3):
                        if i >= 2 and last_of_group(l, i - 2):
                            g = (i - 2) // GROUP[l]
                            act.wait_ge(pv_ready, b * NGROUP + GROUP0[l] + g + 1)
                            if g >= 2:
                                act.wait_ge(ob_ready, b * NGROUP + GROUP0[l] + g - 1)
                            nc.scalar.copy(OT[:, g % 2, :], ps[:, 6, 0:P]).then_inc(ot_evac, 1)
                        if 0 <= i < n:
                            act.wait_ge(pt_ready, b * 2 * NSTEP + 2 * (STEP0[l] + i) + 1)
                            if i >= 8:
                                act.wait_ge(pv_ready, b * NGROUP + GROUP0[l] + (i - 8) // GROUP[l] + 1)
                            nc.scalar.copy(PT[:, i % 8, 0:4, :], ps[:, 4, :].rearrange("p (k q) -> p k q", k=4)
                                           ).then_inc(pt_evacA, 1)
                        s = i + 2
                        if s < n:
                            t, h = s // HEADS[l], s % HEADS[l]
                            act.wait_ge(sum_ready, b * NSTEP + STEP0[l] + s + 1)
                            nc.scalar.activation(T[:, s % 3, :], T[:, s % 3, :], ACT.Exp, bias=nmax[:, t, h:h + 1],
                                                 scale=-1.0, accum_out=rsum[:, t, h:h + 1]).then_inc(exp_ready, 1)
                    if l == 0:
                        def hi_tr(k, dst):
                            act.wait_ge(tr_ready, b * TR + k + 1)
                            nc.scalar.copy(dst, ps[:, 4 + k % 2, :]).then_inc(tr_hi, 1)

                        def square(idx, t):
                            act.wait_ge(res_ready, b * 2 * QT + idx + 1)
                            if idx >= 1:
                                act.wait_ge(sq_ready, b * 2 * QT + idx)
                            nc.scalar.activation(sq[:], O[:, t, :], ACT.Square, scale=float(D) ** -0.5,
                                                 accum_out=stat[:, t, 0:1]).then_inc(sq_ready, 1)

                        for c in range(NC):
                            for k in range(KT):
                                if c > 0 and k == 0:
                                    act.wait_ge(ao_ready, b * QT + c * TPC)
                                hi_tr(c * KT + k, oT[:, 0, k, :])
                            for j in range(TPC):
                                square(c * TPC + j, c * TPC + j)
                        for c in range(NC):
                            for k in range(KT):
                                hi_tr(NC * KT + c * KT + k, x1T[:, c, 0, k, :])
                        for k in range(HU):
                            f = k % FT
                            act.wait_ge(h_ready, b * HU + k + 1)
                            if k >= 2:
                                act.wait_ge(h_lo, b * HU + k - 1)
                            nc.scalar.activation(hs[:, k % 2, :], ps[:, 4 + k % 4, :], ACT.Silu,
                                                 bias=b1c[:, f:f + 1]).then_inc(silu_ready, 1)
                            if k >= 2:
                                act.wait_ge(y_step, b * HU + k - 1)
                            nc.scalar.activation(hT[:, k % 2, 0, :], ps[:, 4 + k % 4, :], ACT.Silu,
                                                 bias=b1c[:, f:f + 1]).then_inc(h_hi, 1)
                            if k >= FT + 2 and k - FT - 2 < TPC:
                                square(QT + k - FT - 2, k - FT - 2)
                        for j in range(TPC):
                            square(QT + TPC + j, TPC + j)

        @block.vector
        def _(dve):
            dve.wait_ge(consts_in, 16 * 8)
            for i in range(NP_):
                dve.wait_ge(w_hi, i + 1)
                nc.vector.tensor_tensor(split_view(i, 1), raw_view(i), f32(split_view(i, 0)),
                                        ALU.subtract).then_inc(w_lo, 1)

            LINKS = QT * 3
            with dve.Fori(0, B) as b:
                chain = [0]

                def link(ins):
                    chain[0] += 1
                    ins.then_inc(dve_step, 1)
                    dve.wait_ge(dve_step, b * LINKS + chain[0])

                for l in (0, 1):
                    for u in range(PROJ):
                        g = l * PROJ + u
                        src = ps[:, g % 8, :]
                        if u < SPLIT:
                            dve.wait_ge(proj_hi, b * 2 * SPLIT + l * SPLIT + u + 1)
                        else:
                            dve.wait_ge(proj_ready, b * 2 * PROJ + g + 1)
                        if u < XT_UNITS:
                            k, c = u // NC, u % NC
                            sl = slice(c * CH, (c + 1) * CH)
                            nc.vector.tensor_tensor(xT[:, 1, k, sl], src, f32(xT[:, 0, k, sl]), ALU.subtract
                                                    ).then_inc(proj_done, 1)
                        elif u < SPLIT:
                            v = u - XT_UNITS
                            m, is_k, c = v // (2 * NC), v // NC % 2, v % NC
                            sl = slice(c * CH, (c + 1) * CH)
                            nc.vector.scalar_tensor_tensor(
                                out=stg[:, is_k, 1, sl], in0=src, scalar=bqk[:, l, is_k, m:m + 1],
                                in1=f32(stg[:, is_k, 0, sl]), op0=ALU.add, op1=ALU.subtract).then_inc(proj_done, 1)
                        else:
                            t = u - SPLIT
                            nc.vector.tensor_tensor(V[:, t, :], src[:, 0:D], bvb[:, l, :], ALU.add).then_inc(proj_done, 1)

                    n = STEPS[l]
                    G, hd, vc = GROUP[l], HD[l], VCOL[l]
                    for i in range(-2, n + 3 + LN_LAG + 1):
                        e = i - 3 - LN_LAG
                        if l == 1 and e >= 0 and e % HEADS[1] == HEADS[1] - 1 and e < n:
                            t = e // HEADS[1]
                            layer_norm(b, O[:, t, :], O[:, t, :], QT + t, t).then_inc(out_ready, 1)
                        if i >= 3 and last_of_group(l, i - 3):
                            g = (i - 3) // G
                            t, h0 = g * G // HEADS[l], g * G % HEADS[l]
                            dve.wait_ge(recip_ready, b * NGROUP + GROUP0[l] + g + 1)
                            dve.wait_ge(ob_ready, b * NGROUP + GROUP0[l] + g + 1)
                            nc.vector.tensor_tensor(
                                O[:, t, h0 * hd:(h0 + G) * hd].rearrange("p (h d) -> p h d", h=G),
                                ps[:, 7, 0:P].rearrange("p (h d) -> p h d", h=G)[:, :, 0:hd],
                                rsum[:, t, h0:h0 + G].unsqueeze(2).to_broadcast([P, G, hd]),
                                ALU.mult).then_inc(norm_done, 1)
                            if l == 1 and (g + 1) % (HEADS[1] // G) == 0:
                                out_stats(b, link, t)
                        if i >= 2 and last_of_group(l, i - 2):
                            g = (i - 2) // G
                            t, h0 = g * G // HEADS[l], g * G % HEADS[l]
                            dve.wait_ge(exp_ready, b * NSTEP + STEP0[l] + i - 1)
                            nc.vector.reciprocal(rsum[:, t, h0:h0 + G], rsum[:, t, h0:h0 + G]).then_inc(recip_ready, 1)
                        s = i + 2
                        if s < n:
                            t, h = s // HEADS[l], s % HEADS[l]
                            if h == 0:
                                if l == 1:
                                    dve.wait_ge(mask_ready, b * QT + t + 1)
                                else:
                                    per = (QT + 2 - t % 3) // 3
                                    dve.wait_ge(adj_in[t % 3], b * 32 * per + 16 * (t // 3 + 1))
                            if s >= 3:
                                dve.wait_ge(pt_ready, b * 2 * NSTEP + 2 * (STEP0[l] + s - 3) + 2)
                            wait_alone(dve, scores_ready, b * NSTEP + STEP0[l] + s + 1)
                            nc.vector.tensor_tensor_reduce(
                                T[:, s % 3, :].rearrange("p (a n) -> p a n", a=2), ps[:, 2 * (s % 2):2 * (s % 2) + 2, :],
                                A[:, t % 3, :].rearrange("p (a n) -> p a n", a=2), -1.0, BIG, ALU.add, ALU.min,
                                nmax[:, t, h:h + 1]).then_inc(sum_ready, 1)
                        if 0 <= i < n:
                            dve.wait_ge(pt_ready, b * 2 * NSTEP + 2 * (STEP0[l] + i) + 2)
                            if i >= 8:
                                dve.wait_ge(pv_ready, b * NGROUP + GROUP0[l] + (i - 8) // G + 1)
                            nc.vector.tensor_copy(PT[:, i % 8, 4:8, :], ps[:, 5, :].rearrange("p (k q) -> p k q", k=4)
                                                  ).then_inc(pt_evacB, 1)
                    if l == 0:
                        feed_forward(b, link)
                assert chain[0] == LINKS, chain[0]

        @block.tensor
        def _(pe):
            pe.wait_ge(consts_ready, 1)

            def split_product(dst, a_hi, a_lo, b_hi, b_lo, first, last):
                pe.matmul(dst, a_hi, b_hi, start=first, stop=False)
                pe.matmul(dst, a_hi, b_lo, start=False, stop=False)
                return pe.matmul(dst, a_lo, b_hi, start=False, stop=last)

            with pe.Fori(0, B) as b:
                for l in (0, 1):
                    for u in range(PROJ):
                        g = l * PROJ + u
                        bank = ps[:, g % 8, :]
                        if u >= 8:
                            pe.wait_ge(proj_done, b * 2 * PROJ + g - 7)
                        elif u == 0:
                            if l == 1:
                                pe.wait_ge(res_ready, b * 2 * QT + 2 * QT)
                            else:
                                pe.wait_ge(w_lo, NP_)
                        if u < XT_UNITS:
                            k, c = u // NC, u % NC
                            for j in range(TPC):
                                t = c * TPC + j
                                if u < NC:
                                    if l == 0:
                                        pe.wait_ge(x_in[t], b * 16 + 16)
                                    else:
                                        pe.wait_ge(x_ready, b * QT + t + 1)
                                mm = pe.transpose(bank[:, j * P:(j + 1) * P], X[:, t, k * P:(k + 1) * P], ident[:])
                        elif u < SPLIT:
                            v = u - XT_UNITS
                            m, is_k, c = v // (2 * NC), v // NC % 2, v % NC
                            i = v // NC
                            if c == 0:
                                per = (2 if i % 4 < 2 else 1)
                                pe.wait_ge(wqk_in[i % 4], b * 32 * per + l * 16 * per + 16 * (i // 4 + 1))
                            if v == 0:
                                pe.wait_ge(proj_done, b * 2 * PROJ + l * PROJ + XT_UNITS)
                            w = wqk[:, i % 4, :].rearrange("p (h k c) -> p h k c", h=2, k=KT)
                            sl = slice(c * CH, (c + 1) * CH)
                            for k in range(KT):
                                mm = split_product(bank, w[:, 0, k, :], w[:, 1, k, :], xT[:, 0, k, sl], xT[:, 1, k, sl],
                                                   k == 0, k == KT - 1)
                        else:
                            t = u - SPLIT
                            if t == 0:
                                pe.wait_ge(wv_in, b * 32 + l * 16 + 16)
                            sl = slice(t * P, (t + 1) * P)
                            for k in range(KT):
                                mm = split_product(bank[:, 0:D], xT[:, 0, k, sl], xT[:, 1, k, sl], wv[:, 0, k, :], wv[:, 1, k, :],
                                                   k == 0, k == KT - 1)
                        mm.then_inc(proj_ready, 1)

                    n, G, vc = STEPS[l], GROUP[l], VCOL[l]
                    for q in range(2):
                        pe.wait_ge(stg_out[q], b * 16 * staged(1, KT - 1, q) + 16 * staged(l, KT - 1, q))
                    pe.wait_ge(proj_done, b * 2 * PROJ + (l + 1) * PROJ)
                    for i in range(-2, n + 3):
                        s = i + 2
                        if s < n:
                            t, h = s // HEADS[l], s % HEADS[l]
                            if s >= 2:
                                pe.wait_ge(sum_ready, b * NSTEP + STEP0[l] + s - 1)
                            q_s = stack(l, 0, h)[:, t * P:(t + 1) * P]
                            for c in range(NC):
                                dst, sl = ps[:, 2 * (s % 2) + c, :], slice(c * CH, (c + 1) * CH)
                                mm = pe.matmul(dst, q_s, stack(l, 1, h)[:, sl], start=True, stop=(l == 1))
                                if l == 0:
                                    mm = pe.matmul(dst, q_s, stack(l, 2, h)[:, sl], start=False, stop=True)
                            mm.then_inc(scores_ready, 1)
                        if 0 <= i < n:
                            pe.wait_ge(exp_ready, b * NSTEP + STEP0[l] + i + 1)
                            for part, evac in ((0, pt_evacA), (1, pt_evacB)):
                                if i >= 1:
                                    pe.wait_ge(evac, b * NSTEP + STEP0[l] + i)
                                for k in range(4):
                                    kk = part * 4 + k
                                    mm = pe.transpose(ps[:, 4 + part, k * P:(k + 1) * P],
                                                      T[:, i % 3, kk * P:(kk + 1) * P], ident[:])
                                mm.then_inc(pt_ready, 1)
                        if i >= 2 and last_of_group(l, i - 2):
                            g = (i - 2) // G
                            pe.wait_ge(ot_evac, b * NGROUP + GROUP0[l] + g + 1)
                            if g >= 1:
                                pe.wait_ge(norm_done, b * NGROUP + GROUP0[l] + g)
                            pe.transpose(ps[:, 7, 0:P], OT[:, g % 2, :], ident[:]).then_inc(ob_ready, 1)
                        if i >= 1 and last_of_group(l, i - 1):
                            g = (i - 1) // G
                            pe.wait_ge(pt_evacA, b * NSTEP + STEP0[l] + i)
                            pe.wait_ge(pt_evacB, b * NSTEP + STEP0[l] + i)
                            if g >= 1:
                                pe.wait_ge(ot_evac, b * NGROUP + GROUP0[l] + g)
                            for k in range(QT):
                                for j in range(G):
                                    s2 = g * G + j
                                    mm = pe.matmul(ps[j * vc:j * vc + HD[l], 6, 0:P], V[:, k, v_cols(l, s2 % HEADS[l])],
                                                   PT[:, s2 % 8, k, :], start=(k == 0), stop=(k == QT - 1))
                            mm.then_inc(pv_ready, 1)

                    if l == 0:
                        pe.wait_ge(norm_done, b * NGROUP + GROUPS[0])
                        for c in range(NC):
                            for k in range(KT):
                                transposed_unit(pe, b, c * KT + k, c, k)
                            if c == 0:
                                pe.wait_ge(wo_in, b * 16 + 16)
                            pe.wait_ge(tr_lo, b * TR + (c + 1) * KT)
                            for j in range(TPC):
                                t = c * TPC + j
                                if t >= 2:
                                    pe.wait_ge(ao_read, b * QT + t - 1)
                                sl = slice(j * P, (j + 1) * P)
                                for k in range(KT):
                                    mm = split_product(ps[:, 6 + t % 2, 0:D], oT[:, 0, k, sl], oT[:, 1, k, sl],
                                                       wos[:, 0, k, :], wos[:, 1, k, :], k == 0, k == KT - 1)
                                mm.then_inc(ao_ready, 1)
                        for c in range(NC):
                            pe.wait_ge(x1_ready, b * QT + (c + 1) * TPC)
                            for k in range(KT):
                                transposed_unit(pe, b, NC * KT + c * KT + k, c, k)

                        def hidden(k):
                            c, f = k // FT, k % FT
                            if f == 0:
                                pe.wait_ge(tr_lo, b * TR + NC * KT + (c + 1) * KT)
                            if c == 0:
                                pe.wait_ge(ff_in[f], b * 16 + 16)
                            if k >= 4:
                                pe.wait_ge(h_hi, b * HU + k - 3)
                            elif k == 0:
                                pe.wait_ge(ao_read, b * QT + QT)
                                pe.wait_ge(tr_lo, b * TR + TR)
                            w = arena[:, f * 2 * half:f * 2 * half + half].rearrange("p (h k c) -> p h k c", h=2, k=KT)
                            for kk in range(KT):
                                mm = split_product(ps[:, 4 + k % 4, :], w[:, 0, kk, :], w[:, 1, kk, :],
                                                   x1T[:, c, 0, kk, :], x1T[:, c, 1, kk, :], kk == 0, kk == KT - 1)
                            mm.then_inc(h_ready, 1)

                        def result(k):
                            c, f = k // FT, k % FT
                            pe.wait_ge(h_lo, b * HU + k + 1)
                            w = arena[:, f * 2 * half + half:(f + 1) * 2 * half].rearrange("p (h n) -> p h n", h=2)
                            for j in range(TPC):
                                if c > 0 and f == 0:
                                    pe.wait_ge(res_ready, b * 2 * QT + QT + (c - 1) * TPC + j + 1)
                                sl = slice(j * P, (j + 1) * P)
                                mm = split_product(ps[:, j, 0:D], hT[:, k % 2, 0, sl], hT[:, k % 2, 1, sl],
                                                   w[:, 0, :], w[:, 1, :], f == 0, f == FT - 1)
                            mm.then_inc(y_step, 1)

                        hidden(0)
                        hidden(1)
                        for k in range(HU):
                            result(k)
                            if k + 2 < HU:
                                hidden(k + 2)

_L0 = ['wq', 'bq', 'wk', 'bk', 'wv', 'bv', 'wo', 'bo', 'w1', 'b1', 'w2', 'b2', 'alpha1', 'gamma1', 'alpha2', 'gamma2']
_L1 = ['Wq', 'bq', 'Wk', 'bk', 'Wv', 'bv', 'beta']
_INS = ['x', 'adj'] + ['L0_gnn_' + n for n in _L0] + ['L1_gnn_' + n for n in _L1]


def kernel(**inputs):
    import numpy as _np
    import concourse.bacc as _bacc
    from concourse import mybir as _mybir
    from concourse.bass_utils import run_bass_kernel_spmd as _run

    nc = _bacc.Bacc("TRN2", target_bir_lowering=False, num_devices=1)
    arrays, args = {}, []
    for name in _INS:
        a = _np.ascontiguousarray(inputs[name])
        if a.ndim == 0:
            a = a.reshape(1)
        arrays[f"in_{name}"] = a
        args.append(nc.dram_tensor(f"in_{name}", a.shape, _mybir.dt.from_np(a.dtype), kind="ExternalInput").ap())
    o = nc.dram_tensor("out_0", (B, N, D), _mybir.dt.float32, kind="ExternalOutput").ap()
    gnn_kernel(nc, *args, o)
    r = _run(nc, [arrays], core_ids=[0])
    return r.results[0]["out_0"]
```

```python
from contextlib import ExitStack

import concourse.bass as bass
from concourse import mybir

F32 = mybir.dt.float32
F32R = mybir.dt.float32r
ALU = mybir.AluOpType
ACT = mybir.ActivationFunctionType

P = 128
B, N, D = 8, 1024, 384
FF = 1536
QT = N // P
KT = D // P
CH = 512
NC = N // CH
TPC = CH // P
FT = FF // P
HEADS = (8, 12)
HD = (D // HEADS[0], D // HEADS[1])
GROUP = (2, 4)
VCOL = (64, 32)
RMS_EPS, LN_EPS = 1e-6, 1e-5
MASKED = -9e15
BIG = 3.0e38

STEPS = [QT * h for h in HEADS]
STEP0 = [0, STEPS[0]]
NSTEP = sum(STEPS)
GROUPS = [STEPS[l] // GROUP[l] for l in (0, 1)]
GROUP0 = [0, GROUPS[0]]
NGROUP = sum(GROUPS)
QK = 2 * KT
UNITS = ([("x", k, 0) for k in range(KT)] + [("qk", u, 0) for u in range(2)] + [("v", t, 0) for t in range(TPC)]
         + [("x", k, 1) for k in range(KT)] + [("qk", u, 1) for u in range(2)]
         + [("qk", u, c) for u in range(2, QK) for c in range(NC)] + [("v", t, 1) for t in range(TPC, QT)])
PROJ = len(UNITS)
SPLIT = PROJ - QT
POOL_TILES = 4
TR = 2 * NC * KT
HU = NC * FT
ROOTS = 4 * QT
AHEAD = 3
TS = AHEAD + 1
PTS = 8
AS = 2
ADJ_USES = QT // AS
STAT_LAG, LN_LAG = 1, 3


def done(kind, i, c):
    return UNITS.index((kind, i, c)) + 1


def bank_of(l, n):
    return (n + 4 * l) % 8


def head_pieces(layer, m):
    hd, out, d = HD[layer], [], m * P
    while d < (m + 1) * P:
        n = min(hd - d % hd, (m + 1) * P - d)
        out.append((d - m * P, d // hd, d % hd, n))
        d += n
    return out


def head_tile(layer, h):
    return ((h + 1) * HD[layer] - 1) // P


def stack_copies(layer, is_k):
    if layer == 0:
        return [(0, 1, 0), (0, 1, 48), (1, 2, 0)] if is_k else [(0, 0, 0), (1, 0, 48)]
    return [(0, 1, 0), (0, 1, 32), (1, 1, 64)] if is_k else [(0, 0, 0), (1, 0, 32), (0, 0, 64)]


HELPED = 3


def stack_dmas(layer, m, is_k):
    out = []
    for row, h, off, n in head_pieces(layer, m):
        for part, blk, at in stack_copies(layer, is_k):
            queue = int(2 * m + is_k < POOL_TILES and len(out) % HELPED == HELPED - 1)
            out.append((row, n, part, blk, h, at + off, queue))
    return out


def staged(layer, m, is_k, queue):
    tiles = ([(0, i) for i in range(KT)] if layer else []) + [(layer, i) for i in range(m + 1)]
    return 16 * sum(d[-1] == queue for l, i in tiles for d in stack_dmas(l, i, is_k))


def gnn_kernel(nc, x, adj, wq0, bq0, wk0, bk0, wv0, bv0, wo, bo, w1, b1, w2, b2, al1, ga1, al2, ga2,
               wq1, bq1, wk1, bk1, wv1, bv1, beta, out):
    with ExitStack() as ctx:
        def sb(name, shape, dt=F32, at=ctx):
            return at.enter_context(nc.sbuf_tensor(name, shape, dt))

        def sem(name):
            return ctx.enter_context(nc.semaphore(name))

        def dram(name, shape):
            return nc.dram_tensor(name, shape, F32, kind="Internal").ap()

        d_qk = dram("split_qk", [2, KT, 2, P, 2 * KT * P])
        d_v = dram("split_v", [2, P, 2 * KT * D])
        d_o = dram("split_o", [P, 2 * KT * D])
        d_ff = dram("split_ff", [FT, P, 2 * 2 * KT * P])

        X = sb("X", [P, QT, D])
        O = sb("O", [P, QT, D])
        V = sb("V", [P, QT, D])
        bvb = sb("bvb", [P, 2, D])
        rowsc = sb("rowsc", [P, 6, D])
        bo_b, b2_b, al1_b, ga1_b, al2_b, ga2_b = (rowsc[:, i, :] for i in range(6))
        small = sb("small", [P, 4 * KT + FT + 4])
        bqk = small[:, 0:4 * KT].rearrange("p (l w m) -> p l w m", l=2, w=2)
        b1c = small[:, 4 * KT:4 * KT + FT]
        betac, powc, epsr, epsl = (small[:, 4 * KT + FT + i:4 * KT + FT + i + 1] for i in range(4))
        ident = sb("ident", [P, P])
        nmax = sb("nmax", [P, QT, HEADS[1]])
        rsum = sb("rsum", [P, QT, HEADS[1]])
        OT = sb("OT", [P, 2, P])
        stat = sb("stat", [P, QT, 13])
        arena = sb("arena", [P, 24 * N], F32R)

        proj = ExitStack()
        stg = sb("stg", [P, 2, 2, N], F32R, proj)
        xT = sb("xT", [P, 2, KT, N], F32R, proj)
        wv = sb("wv", [P, 2, KT, D], F32R, proj)
        wqk = sb("wqk", [P, 4, 2 * KT * P], F32R, proj)
        proj.close()
        attn = ExitStack()
        PT = sb("PT", [P, PTS, QT, P], at=attn)
        T = sb("T", [P, TS, N], at=attn)
        sb("below_wqk", [P, P + P], at=attn)
        maskt = sb("maskt", [P, N], at=attn)
        A = sb("A", [P, AS, N], at=attn)
        attn.close()
        ffn = ExitStack()
        hT = sb("hT", [P, 2, 2, CH], F32R, ffn)
        hs = sb("hs", [P, 2, CH], at=ffn)
        sq = sb("sq", [P, D], at=ffn)
        xT1 = sb("xT1", [P, NC, 2, KT, CH], F32R, ffn)
        sb("below_wos", [P, 49 * 256 - (4 * CH + 2 * CH + D + NC * 2 * KT * CH)], at=ffn)
        wos = sb("wos", [P, 2, KT, D], F32R, ffn)
        ffn.close()

        ps = ctx.enter_context(nc.psum_tensor("ps", [P, 8, CH], F32))

        def f32(ap):
            return ap.bitcast(F32)

        raw = [r_.rearrange("p k n -> p (k n)") for r_ in (V[:, 0:KT, :], V[:, KT:2 * KT, :], O[:, 0:KT, :])]

        consts_in = sem("consts_in")
        bias_in = sem("bias_in")
        ident_zero = sem("ident_zero")
        consts_ready = sem("consts_ready")
        pconst_ready = sem("pconst_ready")
        raw_in = [sem(f"raw_in{i}") for i in range(3)]
        w_scaled = sem("w_scaled")
        w_hi = sem("w_hi")
        w_lo = sem("w_lo")
        split_out = [sem(f"split_out{i}") for i in range(3)]
        x_in = [sem(f"x_in{t}") for t in range(QT)]
        wqk_in = [sem(f"wqk_in{i}") for i in range(4)]
        wv_in = sem("wv_in")
        proj_ready = sem("proj_ready")
        proj_hi = sem("proj_hi")
        proj_done = sem("proj_done")
        stacked = [[sem(f"stacked_{w}_{e}") for w in "qk"] for e in ("sync", "gpsimd")]
        adj_in = [sem(f"adj_in{i}") for i in range(AS)]
        mask_step = sem("mask_step")
        mask_ready = sem("mask_ready")
        scores_ready = sem("scores_ready")
        sum_ready = sem("sum_ready")
        exp_ready = sem("exp_ready")
        pt_ready = sem("pt_ready")
        pt_evacA = sem("pt_evacA")
        pt_evacB = sem("pt_evacB")
        pv_ready = sem("pv_ready")
        ot_evac = sem("ot_evac")
        ob_ready = sem("ob_ready")
        recip_ready = sem("recip_ready")
        norm_done = sem("norm_done")
        wo_in = sem("wo_in")
        ff_in = [sem(f"ff_in{f}") for f in range(FT)]
        tr_ready = sem("tr_ready")
        tr_hi = sem("tr_hi")
        tr_lo = sem("tr_lo")
        ao_ready = sem("ao_ready")
        pre1_ready = sem("pre1_ready")
        res_ready = sem("res_ready")
        sq_ready = sem("sq_ready")
        x1_ready = sem("x1_ready")
        dve_step = sem("dve_step")
        rms_ready = sem("rms_ready")
        stats_step = sem("stats_step")
        waits_passed = sem("waits_passed")
        var_ready = sem("var_ready")
        ln_ready = sem("ln_ready")
        root_step = sem("root_step")
        pool_step = sem("pool_step")
        pre2_ready = sem("pre2_ready")
        h_ready = sem("h_ready")
        silu_ready = sem("silu_ready")
        h_hi = sem("h_hi")
        h_lo = sem("h_lo")
        y_step = sem("y_step")
        y_read = sem("y_read")
        x_ready = sem("x_ready")
        r1_ready = sem("r1_ready")
        x_free = sem("x_free")
        out_ready = sem("out_ready")
        out_done = [sem(f"out_done{t}") for t in range(QT)]

        def rows(w):
            return w.rearrange("(k p) n -> p k n", p=P)

        PIECES = []
        for l, (wq_, wk_, wv_) in enumerate(((wq0, wk0, wv0), (wq1, wk1, wv1))):
            PIECES.append((rows(wq_), float(HD[l]) ** -0.5, [d_qk[l, m, 0] for m in range(KT)], "cols"))
            PIECES.append((rows(wk_), None, [d_qk[l, m, 1] for m in range(KT)], "cols"))
            PIECES.append((rows(wv_), None, [d_v[l]], "rows"))
        PIECES.append((rows(wo), None, [d_o], "rows"))
        half = 2 * KT * P
        for i in range(FT // KT):
            fs = range(i * KT, (i + 1) * KT)
            PIECES.append((rows(w1)[:, :, i * D:(i + 1) * D], None, [d_ff[f][:, 0:half] for f in fs], "cols"))
            PIECES.append((rows(w2)[:, i * KT:(i + 1) * KT, :], None, [d_ff[f][:, half:2 * half] for f in fs], "tiles"))
        NP_ = len(PIECES)
        PW = 2 * KT * D

        def split_view(i, part):
            s = arena[:, (i % 3) * PW:(i % 3 + 1) * PW]
            kind = PIECES[i][3]
            if kind == "cols":
                return s.rearrange("p (m h k c) -> p h k m c", m=KT, h=2, k=KT)[:, part]
            if kind == "rows":
                return s.rearrange("p (h k n) -> p h k n", h=2, k=KT)[:, part]
            return s.rearrange("p (f h n) -> p h f n", f=KT, h=2)[:, part]

        def raw_view(i):
            v = raw[i % 3]
            if PIECES[i][3] == "cols":
                return v.rearrange("p (k m c) -> p k m c", k=KT, m=KT)
            return v.rearrange("p (k n) -> p k n", k=KT)

        def all_split(q):
            return 16 * sum(piece_outs(j) for j in range(q, NP_, 3))

        def piece_outs(i):
            return len(PIECES[i][2])

        def outs_before(i):
            return sum(piece_outs(j) for j in range(i % 3, i + 1, 3))

        def stack(layer, block, h):
            c = (block * HEADS[layer] + h) * N
            return arena[0:96, c:c + N]

        def v_cols(layer, h):
            return slice(h * HD[layer], (h + 1) * HD[layer])

        def last_of_group(layer, s):
            return s < STEPS[layer] and s % GROUP[layer] == GROUP[layer] - 1

        def wait_alone(eng, sem_, value):
            eng.wait_ge(sem_, value)
            eng.sem_inc(waits_passed, 1)

        def first_weights(sp, l):
            for u in range(4):
                sp.dma_start(f32(wqk[:, u, :]), d_qk[l, u // 2, u % 2]).then_inc(wqk_in[u], 16)
            sp.dma_start(f32(wv[:]).rearrange("p h k n -> p (h k n)"), d_v[l]).then_inc(wv_in, 16)

        def store_and_next(sp, b, t):
            sp.wait_ge(x_free, b * QT + t + 1)
            nb = (b + 1) % B
            sp.dma_start(X[:, t, :], x[nb, t * P:(t + 1) * P, :]).then_inc(x_in[t], 16)
            sp.wait_ge(out_ready, b * QT + t + 1)
            sp.dma_start(out[b, t * P:(t + 1) * P, :], O[:, t, :]).then_inc(out_done[t], 16)

        def copy_stacks(eng, b, l, u, mine):
            m, is_k = u // 2, u % 2
            wait_alone(eng, proj_done, b * 2 * PROJ + l * PROJ + done("qk", u, 1))
            for row, n, part, blk, h, at, queue in stack_dmas(l, m, is_k):
                if queue == mine:
                    dst = arena[at:at + n, (blk * HEADS[l] + h) * N:(blk * HEADS[l] + h + 1) * N]
                    eng.dma_start(f32(dst), f32(stg[row:row + n, is_k, part, :])).then_inc(stacked[queue][is_k], 16)

        def wait_stacks(eng, b, l, m, is_k):
            for queue in range(2):
                eng.wait_ge(stacked[queue][is_k], b * staged(1, KT - 1, is_k, queue) + staged(l, m, is_k, queue))

        def adj_rows(t):
            return A[:, (t + 1) % AS, :]

        def pt_slot(i):
            return (i + PTS // 2) % PTS

        def acts_b(l, i):
            return l == 1 and i % 4 == 1

        def rms(link, b, idx, t, gain):
            nc.vector.wait_ge(rms_ready, b * 2 * QT + idx + 1)
            link(nc.vector.scalar_tensor_tensor(out=O[:, t, :], in0=O[:, t, :], scalar=stat[:, t, 2:3], in1=gain,
                                                op0=ALU.mult, op1=ALU.mult))

        def layer_stats(b, src, idx, t):
            nc.vector.bn_stats(stat[:, t, 4:10], src).then_inc(stats_step, 1)
            wait_alone(nc.vector, stats_step, b * 2 * QT + idx + 1)
            nc.vector.bn_aggr(stat[:, t, 10:12], stat[:, t, 4:10]).then_inc(var_ready, 1)

        def layer_norm(b, src, dst, idx, t):
            nc.vector.wait_ge(ln_ready, b * 2 * QT + idx + 1)
            return nc.vector.tensor_scalar(dst, src, stat[:, t, 10:11], stat[:, t, 12:13], ALU.subtract, ALU.mult)

        def inverse_root(pool, b, n, src, eps, dst):
            nc.gpsimd.tensor_tensor(src, src, eps, ALU.add).then_inc(root_step, 1)
            pool.wait_ge(root_step, b * ROOTS + n)
            return nc.gpsimd.tensor_tensor(dst, src, powc, ALU.pow)

        def lo_tr(dve, b, k):
            c, kt = k % (NC * KT) // KT, k % KT
            dve.wait_ge(tr_hi, b * TR + k + 1)
            dve.tensor_tensor(xT1[:, c, 1, kt, :], ps[:, tr_bank(k), :], f32(xT1[:, c, 0, kt, :]), ALU.subtract
                              ).then_inc(tr_lo, 1)

        def tail_sum(dve, b, t):
            dve.wait_ge(pre2_ready, b * QT + t + 1)
            dve.wait_ge(y_step, b * HU + (t // TPC + 1) * FT)
            dve.tensor_tensor(O[:, t, :], ps[:, t % TPC, 0:D], O[:, t, :], ALU.add).then_inc(res_ready, 1)

        def tail_norms(dve, b, link, t):
            rms(link, b, QT + t, t, al2_b)
            dve.wait_ge(pool_step, b * QT + t + 1)
            link(dve.tensor_tensor(O[:, t, :], O[:, t, :], X[:, t, :], ALU.add))
            layer_stats(b, O[:, t, :], t, t)

        def tail_end(dve, b, t):
            layer_norm(b, O[:, t, :], X[:, t, :], t, t).then_inc(x_ready, 1)

        def feed_forward(b, link):
            dve = nc.vector
            for k in range(NC * KT):
                lo_tr(dve, b, k)

            def x1(t):
                rms(link, b, t, t, al1_b)
                dve.tensor_tensor(O[:, t, :], O[:, t, :], ga1_b, ALU.add).then_inc(x1_ready, 1)

            for t in range(QT):
                dve.wait_ge(pre1_ready, b * QT + t + 1)
                dve.wait_ge(ao_ready, b * QT + t + 1)
                dve.tensor_tensor(O[:, t, :], ps[:, ao_bank(t), 0:D], O[:, t, :], ALU.add).then_inc(res_ready, 1)
                if t >= 2:
                    x1(t - 2)
                if t == QT - 2:
                    for k in range(KT):
                        lo_tr(dve, b, NC * KT + k)
            for t in range(QT - 2, QT):
                x1(t)

            for k in range(HU):
                dve.wait_ge(silu_ready, b * HU + k + 1)
                dve.wait_ge(h_hi, b * HU + k + 1)
                dve.tensor_tensor(hT[:, k % 2, 1, :], hs[:, k % 2, :], f32(hT[:, k % 2, 0, :]), ALU.subtract
                                  ).then_inc(h_lo, 1)
                if 2 <= k < 2 + KT:
                    lo_tr(dve, b, NC * KT + KT + k - 2)
                if k == FT:
                    for t in range(TPC):
                        tail_sum(dve, b, t)
                if k >= FT + 3 and k - FT - 3 < TPC:
                    tail_norms(dve, b, link, k - FT - 3)
                if k >= FT + 7 and k - FT - 7 < TPC:
                    tail_end(dve, b, k - FT - 7)
            for t in range(TPC, QT):
                tail_sum(dve, b, t)

        def tr_bank(k):
            if k < NC * KT:
                return k
            return (7, 0, 1)[k % KT] if k < NC * KT + KT else 7

        def ao_bank(t):
            return (6 + t) % 8

        def out_stats(b, t):
            nc.vector.wait_ge(x_free, b * QT + t + 1)
            layer_stats(b, O[:, t, :], QT + t, t)

        def transposed_unit(pe, k):
            c, kt = k % (NC * KT) // KT, k % KT
            for j in range(TPC):
                mm = pe.transpose(ps[:, tr_bank(k), j * P:(j + 1) * P], O[:, c * TPC + j, kt * P:(kt + 1) * P], ident[:])
            mm.then_inc(tr_ready, 1)

        block = ctx.enter_context(nc.Block())

        @block.sync
        def _(sp):
            for t in range(QT):
                sp.dma_start(X[:, t, :], x[0, t * P:(t + 1) * P, :]).then_inc(x_in[t], 16)
            for i in range(NP_ + 2):
                if i < NP_:
                    if i >= 3:
                        sp.wait_ge(w_lo, i - 2)
                    sp.dma_start(raw[i % 3].rearrange("p (k n) -> p k n", k=KT), PIECES[i][0]).then_inc(raw_in[i % 3], 16)
                j = i - 2
                if j >= 0:
                    sp.wait_ge(w_lo, j + 1)
                    s = arena[:, (j % 3) * PW:(j % 3 + 1) * PW].rearrange("p (d n) -> p d n", d=piece_outs(j))
                    for d, dst in enumerate(PIECES[j][2]):
                        sp.dma_start(dst, f32(s[:, d, :])).then_inc(split_out[j % 3], 16)
            for q in range(3):
                sp.wait_ge(split_out[q], 16 * piece_outs(q))
            first_weights(sp, 0)
            for q in range(3):
                sp.wait_ge(split_out[q], all_split(q))

            with sp.Fori(0, B) as b:
                for l in (0, 1):
                    if l == 1:
                        sp.wait_ge(ao_ready, b * QT + QT)
                        first_weights(sp, l)
                    for u in range(QK):
                        copy_stacks(sp, b, l, u, 0)
                        if u + 4 < QK:
                            sp.wait_ge(proj_ready, b * 2 * PROJ + l * PROJ + done("qk", u, 1))
                            sp.dma_start(f32(wqk[:, u, :]), d_qk[l, (u + 4) // 2, u % 2]).then_inc(wqk_in[u], 16)
                        if u == 3:
                            sp.dma_start(adj_rows(0), adj[b, 0:P, :]).then_inc(adj_in[0], 16)
                    for t in range(1, QT):
                        if t >= AS:
                            sp.wait_ge(sum_ready, b * NSTEP + STEP0[l] + (t - AS + 1) * HEADS[l])
                        sp.dma_start(adj_rows(t), adj[b, t * P:(t + 1) * P, :]).then_inc(adj_in[t % AS], 16)
                        if l == 1 and t >= 3:
                            store_and_next(sp, b, t - 3)
                    if l == 0:
                        sp.wait_ge(sum_ready, b * NSTEP + STEPS[0])
                        sp.dma_start(f32(wos[:]).rearrange("p h k n -> p (h k n)"), d_o).then_inc(wo_in, 16)
                        sp.wait_ge(scores_ready, b * NSTEP + STEPS[0])
                        for f in range(FT):
                            w = 2 * half
                            sp.dma_start(f32(arena[:, f * w:(f + 1) * w]), d_ff[f]).then_inc(ff_in[f], 16)
                    else:
                        store_and_next(sp, b, QT - 3)
                        sp.wait_ge(sum_ready, b * NSTEP + NSTEP)
                        wait_alone(sp, pt_ready, b * 2 * NSTEP + 2 * NSTEP)
                        first_weights(sp, 0)
                        for t in range(QT - 2, QT):
                            store_and_next(sp, b, t)
                        for t in range(QT):
                            wait_alone(sp, out_done[t], b * 16 + 16)
            for i in range(4):
                sp.wait_ge(wqk_in[i], 16 * (2 * B * (2 if i < 2 else 1) + 1))
            sp.wait_ge(wv_in, 16 * (2 * B + 1))
            for t in range(QT):
                sp.wait_ge(x_in[t], 16 * (B + 1))

        @block.gpsimd
        def _(pool):
            nc.gpsimd.memset(ident[:], 0.0).then_inc(ident_zero, 1)
            pool.wait_ge(ident_zero, 1)
            nc.gpsimd.affine_select(out=ident[:], in_=ident[:], compare_op=ALU.not_equal, fill=1.0, base=0,
                                    pattern=[[-1, P]], channel_multiplier=1).then_inc(consts_ready, 1)
            nc.gpsimd.memset(powc, -0.5).then_inc(pconst_ready, 1)
            nc.gpsimd.memset(epsr, RMS_EPS).then_inc(pconst_ready, 1)
            nc.gpsimd.memset(epsl, LN_EPS).then_inc(pconst_ready, 1)
            for i, r in enumerate((bo, b2, al1, ga1, al2, ga2)):
                pool.dma_start(rowsc[:, i, :], r.partition_broadcast(P)).then_inc(consts_in, 16)
            for i, r in enumerate((bv0, bv1)):
                pool.dma_start(bvb[:, i, :], r.partition_broadcast(P)).then_inc(consts_in, 16)
            for i, r in enumerate((bq0, bk0, bq1, bk1)):
                pool.dma_start(bqk[:, i // 2, i % 2, :], r.rearrange("(m p) -> p m", p=P),
                               allow_slow_non_contiguous=True).then_inc(bias_in, 16)
            pool.dma_start(b1c, b1.rearrange("(m p) -> p m", p=P), allow_slow_non_contiguous=True).then_inc(bias_in, 16)
            pool.dma_start(betac, beta.partition_broadcast(P)).then_inc(bias_in, 16)
            pool.wait_ge(consts_in, 16 * 8)
            pool.wait_ge(bias_in, 16 * 6)
            pool.wait_ge(pconst_ready, 3)

            for q in range(3):
                pool.wait_ge(split_out[q], all_split(q))

            with pool.Fori(0, B) as b:
                for u in range(POOL_TILES):
                    copy_stacks(pool, b, 0, u, 1)

                def x_plus_bo(t):
                    pool.wait_ge(tr_ready, b * TR + (t // TPC + 1) * KT)
                    nc.gpsimd.tensor_tensor(O[:, t, :], X[:, t, :], bo_b, ALU.add).then_inc(pre1_ready, 1)

                for t in range(QT - 2):
                    x_plus_bo(t)
                for t in range(QT):
                    pool.wait_ge(sq_ready, b * 2 * QT + t + 1)
                    inverse_root(pool, b, t + 1, stat[:, t, 0:1], epsr, stat[:, t, 2:3]).then_inc(rms_ready, 1)
                    if t < 2:
                        x_plus_bo(QT - 2 + t)
                for t in range(QT):
                    nc.gpsimd.tensor_tensor(X[:, t, :], X[:, t, :], ga2_b, ALU.add).then_inc(pool_step, 1)
                for t in range(QT):
                    pool.wait_ge(tr_ready, b * TR + NC * KT + (t // TPC + 1) * KT)
                    nc.gpsimd.tensor_tensor(O[:, t, :], O[:, t, :], b2_b, ALU.add).then_inc(pre2_ready, 1)
                n = QT
                for c in range(NC):
                    for t in range(c * TPC, (c + 1) * TPC):
                        n += 1
                        pool.wait_ge(sq_ready, b * 2 * QT + QT + t + 1)
                        inverse_root(pool, b, n, stat[:, t, 0:1], epsr, stat[:, t, 2:3]).then_inc(rms_ready, 1)
                    for t in range(c * TPC, (c + 1) * TPC):
                        n += 1
                        pool.wait_ge(var_ready, b * 2 * QT + t + 1)
                        inverse_root(pool, b, n, stat[:, t, 11:12], epsl, stat[:, t, 12:13]).then_inc(ln_ready, 1)
                for u in range(POOL_TILES):
                    copy_stacks(pool, b, 1, u, 1)
                for t in range(QT + 2):
                    if t < QT:
                        m = O[:, QT - 3:QT, :].rearrange("p t n -> p (t n)")[:, 0:N] if t == 0 else maskt[:]
                        if t == 1:
                            pool.wait_ge(proj_ready, b * 2 * PROJ + PROJ + done("qk", QK - 1, 1))
                        elif t > 1:
                            pool.wait_ge(mask_ready, b * QT + t)
                        wait_alone(pool, adj_in[t % AS], b * 32 * ADJ_USES + 16 * (ADJ_USES + t // AS + 1))
                        nc.gpsimd.tensor_scalar(m, adj_rows(t), 0.0, MASKED, ALU.is_le, ALU.mult).then_inc(mask_step, 1)
                        wait_alone(pool, mask_step, b * 2 * QT + 2 * t + 1)
                        nc.gpsimd.tensor_scalar(adj_rows(t), adj_rows(t), betac[:, 0:1], None, ALU.mult).then_inc(mask_step, 1)
                        pool.wait_ge(mask_step, b * 2 * QT + 2 * t + 2)
                        nc.gpsimd.tensor_tensor(adj_rows(t), adj_rows(t), m, ALU.add).then_inc(mask_ready, 1)
                    if t >= 2:
                        pool.wait_ge(norm_done, b * NGROUP + GROUP0[1] + (t - 1) * (HEADS[1] // GROUP[1]))
                        nc.gpsimd.tensor_tensor(O[:, t - 2, :], O[:, t - 2, :], X[:, t - 2, :], ALU.add).then_inc(x_free, 1)
                        pool.wait_ge(var_ready, b * 2 * QT + QT + t - 1)
                        inverse_root(pool, b, 3 * QT + t - 1, stat[:, t - 2, 11:12], epsl,
                                     stat[:, t - 2, 12:13]).then_inc(ln_ready, 1)

        @block.scalar
        def _(act):
            act.wait_ge(bias_in, 16 * 6)
            for l in (0, 1):
                nc.scalar.mul(bqk[:, l, 0, :], bqk[:, l, 0, :], float(HD[l]) ** -0.5).then_inc(w_scaled, 1)
            scaled = 2
            for i in range(NP_):
                act.wait_ge(raw_in[i % 3], 16 * (i // 3 + 1))
                if PIECES[i][1] is not None:
                    nc.scalar.mul(raw[i % 3], raw[i % 3], PIECES[i][1]).then_inc(w_scaled, 1)
                    scaled += 1
                    act.wait_ge(w_scaled, scaled)
                if i >= 3:
                    act.wait_ge(split_out[i % 3], 16 * outs_before(i - 3))
                nc.scalar.copy(split_view(i, 0), raw_view(i)).then_inc(w_hi, 1)

            with act.Fori(0, B) as b:
                for l in (0, 1):
                    for n, (kind, i, c) in enumerate(UNITS):
                        if kind == "v":
                            continue
                        act.wait_ge(proj_ready, b * 2 * PROJ + l * PROJ + n + 1)
                        src, sl = ps[:, bank_of(l, n), :], slice(c * CH, (c + 1) * CH)
                        if kind == "x":
                            nc.scalar.copy(xT[:, 0, i, sl], src).then_inc(proj_hi, 1)
                        else:
                            m, is_k = i // 2, i % 2
                            if c == 0 and m > 0:
                                wait_stacks(act, b, l, m - 1, is_k)
                            nc.scalar.activation(stg[:, is_k, 0, sl], src, ACT.Identity,
                                                 bias=bqk[:, l, is_k, m:m + 1]).then_inc(proj_hi, 1)

                    n = STEPS[l]
                    for i in range(-2, n + GROUP[l] + 2):
                        if i > GROUP[l] and last_of_group(l, i - GROUP[l] - 1):
                            g = (i - GROUP[l] - 1) // GROUP[l]
                            act.wait_ge(pv_ready, b * NGROUP + GROUP0[l] + g + 1)
                            if g >= 2:
                                act.wait_ge(ob_ready, b * NGROUP + GROUP0[l] + g - 1)
                            nc.scalar.copy(OT[:, g % 2, :], ps[:, 6 + g % 2, 0:P]).then_inc(ot_evac, 1)
                        if 0 <= i < n:
                            act.wait_ge(pt_ready, b * 2 * NSTEP + 2 * (STEP0[l] + i) + 1)
                            if i >= PTS:
                                act.wait_ge(pv_ready, b * NGROUP + GROUP0[l] + (i - PTS) // GROUP[l] + 1)
                            if i == PTS // 2:
                                for q in range(2):
                                    wait_stacks(act, b, l, KT - 1, q)
                            nc.scalar.copy(PT[:, pt_slot(i), 0:4, :], ps[:, 4, :].rearrange("p (k q) -> p k q", k=4)
                                           ).then_inc(pt_evacA, 1)
                            if acts_b(l, i):
                                act.wait_ge(pt_ready, b * 2 * NSTEP + 2 * (STEP0[l] + i) + 2)
                                nc.scalar.copy(PT[:, pt_slot(i), 4:8, :], ps[:, 5, :].rearrange("p (k q) -> p k q", k=4)
                                               ).then_inc(pt_evacB, 1)
                        s = i + 2
                        if s < n:
                            t, h = s // HEADS[l], s % HEADS[l]
                            act.wait_ge(sum_ready, b * NSTEP + STEP0[l] + s + 1)
                            nc.scalar.activation(T[:, s % TS, :], T[:, s % TS, :], ACT.Exp, bias=nmax[:, t, h:h + 1],
                                                 scale=-1.0, accum_out=rsum[:, t, h:h + 1]).then_inc(exp_ready, 1)
                    if l == 0:
                        def hi_tr(k):
                            act.wait_ge(tr_ready, b * TR + k + 1)
                            nc.scalar.copy(xT1[:, k % (NC * KT) // KT, 0, k % KT, :], ps[:, tr_bank(k), :]).then_inc(tr_hi, 1)

                        def square(idx, t):
                            act.wait_ge(res_ready, b * 2 * QT + idx + 1)
                            if idx >= 1:
                                act.wait_ge(sq_ready, b * 2 * QT + idx)
                            nc.scalar.activation(sq[:], O[:, t, :], ACT.Square, scale=float(D) ** -0.5,
                                                 accum_out=stat[:, t, 0:1]).then_inc(sq_ready, 1)

                        for k in range(NC * KT):
                            hi_tr(k)
                        for t in range(QT):
                            if t == QT - 1:
                                for k in range(KT):
                                    hi_tr(NC * KT + k)
                            square(t, t)
                        for k in range(HU):
                            f = k % FT
                            bank = ps[:, 4 + k % 3, :]
                            act.wait_ge(h_ready, b * HU + k + 1)
                            if k >= 2:
                                act.wait_ge(h_lo, b * HU + k - 1)
                            nc.scalar.activation(hs[:, k % 2, :], bank, ACT.Silu, bias=b1c[:, f:f + 1]).then_inc(silu_ready, 1)
                            if k >= 2:
                                act.wait_ge(y_step, b * HU + k - 1)
                            nc.scalar.activation(hT[:, k % 2, 0, :], bank, ACT.Silu, bias=b1c[:, f:f + 1]).then_inc(h_hi, 1)
                            if 2 <= k < 2 + KT:
                                hi_tr(NC * KT + KT + k - 2)
                            if k >= FT + 2 and k - FT - 2 < TPC:
                                square(QT + k - FT - 2, k - FT - 2)
                        for j in range(TPC):
                            square(QT + TPC + j, TPC + j)

        @block.vector
        def _(dve):
            dve.wait_ge(consts_in, 16 * 8)
            for i in range(NP_):
                dve.wait_ge(w_hi, i + 1)
                nc.vector.tensor_tensor(split_view(i, 1), raw_view(i), f32(split_view(i, 0)),
                                        ALU.subtract).then_inc(w_lo, 1)

            LINKS = QT * 3
            with dve.Fori(0, B) as b:
                chain = [0]

                def link(ins):
                    chain[0] += 1
                    ins.then_inc(dve_step, 1)
                    dve.wait_ge(dve_step, b * LINKS + chain[0])

                for l in (0, 1):
                    tail = {3: [(tail_norms, 4)], 4: [(tail_norms, 5)], 5: [(tail_norms, 6)], 6: [(tail_norms, 7)],
                            7: [(tail_end, 4)], 8: [(tail_end, 5)], 9: [(tail_end, 6), (tail_end, 7)]}
                    hi = 0
                    for n, (kind, i, c) in enumerate(UNITS):
                        if l == 1:
                            for part, t in tail.get(n, []):
                                if part is tail_norms:
                                    tail_norms(dve, b, link, t)
                                else:
                                    tail_end(dve, b, t)
                        src, sl = ps[:, bank_of(l, n), :], slice(c * CH, (c + 1) * CH)
                        if kind == "v":
                            dve.wait_ge(proj_ready, b * 2 * PROJ + l * PROJ + n + 1)
                            nc.vector.tensor_tensor(V[:, i, :], src[:, 0:D], bvb[:, l, :], ALU.add).then_inc(proj_done, 1)
                            continue
                        hi += 1
                        dve.wait_ge(proj_hi, b * 2 * SPLIT + l * SPLIT + hi)
                        if kind == "x":
                            nc.vector.tensor_tensor(xT[:, 1, i, sl], src, f32(xT[:, 0, i, sl]), ALU.subtract
                                                    ).then_inc(proj_done, 1)
                        else:
                            m, is_k = i // 2, i % 2
                            nc.vector.scalar_tensor_tensor(
                                out=stg[:, is_k, 1, sl], in0=src, scalar=bqk[:, l, is_k, m:m + 1],
                                in1=f32(stg[:, is_k, 0, sl]), op0=ALU.add, op1=ALU.subtract).then_inc(proj_done, 1)

                    n = STEPS[l]
                    G, hd, vc = GROUP[l], HD[l], VCOL[l]
                    for i in range(-AHEAD, n + G + 2 + LN_LAG + 1):
                        s = i + AHEAD
                        if s < n:
                            t, h = s // HEADS[l], s % HEADS[l]
                            if h == 0:
                                if l == 1:
                                    dve.wait_ge(mask_ready, b * QT + t + 1)
                                else:
                                    dve.wait_ge(adj_in[t % AS], b * 32 * ADJ_USES + 16 * (t // AS + 1))
                            if s >= TS:
                                dve.wait_ge(pt_ready, b * 2 * NSTEP + 2 * (STEP0[l] + s - TS) + 2)
                            wait_alone(dve, scores_ready, b * NSTEP + STEP0[l] + s + 1)
                            nc.vector.tensor_tensor_reduce(
                                T[:, s % TS, :].rearrange("p (a n) -> p a n", a=2), ps[:, 2 * (s % 2):2 * (s % 2) + 2, :],
                                adj_rows(t).rearrange("p (a n) -> p a n", a=2), -1.0, BIG, ALU.add, ALU.min,
                                nmax[:, t, h:h + 1]).then_inc(sum_ready, 1)
                        if 0 <= i < n and not acts_b(l, i):
                            dve.wait_ge(pt_ready, b * 2 * NSTEP + 2 * (STEP0[l] + i) + 2)
                            if i >= PTS:
                                dve.wait_ge(pv_ready, b * NGROUP + GROUP0[l] + (i - PTS) // G + 1)
                            if i == PTS // 2:
                                for q in range(2):
                                    wait_stacks(dve, b, l, KT - 1, q)
                            nc.vector.tensor_copy(PT[:, pt_slot(i), 4:8, :], ps[:, 5, :].rearrange("p (k q) -> p k q", k=4)
                                                  ).then_inc(pt_evacB, 1)
                        if i >= 2 and last_of_group(l, i - 2):
                            g = (i - 2) // G
                            t, h0 = g * G // HEADS[l], g * G % HEADS[l]
                            dve.wait_ge(exp_ready, b * NSTEP + STEP0[l] + i - 1)
                            nc.vector.reciprocal(rsum[:, t, h0:h0 + G], rsum[:, t, h0:h0 + G]).then_inc(recip_ready, 1)
                        if i >= G + 2 and last_of_group(l, i - G - 2):
                            g = (i - G - 2) // G
                            t, h0 = g * G // HEADS[l], g * G % HEADS[l]
                            dve.wait_ge(recip_ready, b * NGROUP + GROUP0[l] + g + 1)
                            dve.wait_ge(ob_ready, b * NGROUP + GROUP0[l] + g + 1)
                            nc.vector.tensor_tensor(
                                O[:, t, h0 * hd:(h0 + G) * hd].rearrange("p (h d) -> p h d", h=G),
                                ps[:, 6 + g % 2, 0:P].rearrange("p (h d) -> p h d", h=G)[:, :, 0:hd],
                                rsum[:, t, h0:h0 + G].unsqueeze(2).to_broadcast([P, G, hd]),
                                ALU.mult).then_inc(norm_done, 1)
                        if l == 1:
                            for lag, part in ((STAT_LAG, out_stats), (LN_LAG, layer_norm)):
                                e = i - G - 2 - lag
                                if 0 <= e < n and e % HEADS[1] == HEADS[1] - 1:
                                    t = e // HEADS[1]
                                    if part is out_stats:
                                        out_stats(b, t)
                                    else:
                                        layer_norm(b, O[:, t, :], O[:, t, :], QT + t, t).then_inc(out_ready, 1)
                    if l == 0:
                        feed_forward(b, link)
                assert chain[0] == LINKS, chain[0]

        @block.tensor
        def _(pe):
            pe.wait_ge(consts_ready, 1)

            def split_product(dst, a_hi, a_lo, b_hi, b_lo, first, last):
                pe.matmul(dst, a_hi, b_hi, start=first, stop=False)
                pe.matmul(dst, a_hi, b_lo, start=False, stop=False)
                return pe.matmul(dst, a_lo, b_hi, start=False, stop=last)

            with pe.Fori(0, B) as b:
                for l in (0, 1):
                    for n, (kind, i, c) in enumerate(UNITS):
                        at = bank_of(l, n)
                        bank = ps[:, at, :]
                        if n >= 8:
                            pe.wait_ge(proj_done, b * 2 * PROJ + l * PROJ + n - 7)
                        elif l == 1:
                            if at >= 4 and n == 0:
                                pe.wait_ge(h_hi, b * HU + HU)
                            elif at < 4:
                                pe.wait_ge(res_ready, b * 2 * QT + QT + TPC + at + 1)
                        if kind == "x":
                            for j in range(TPC):
                                t = c * TPC + j
                                if i == 0:
                                    if l == 0:
                                        pe.wait_ge(x_in[t], b * 16 + 16)
                                    else:
                                        pe.wait_ge(x_ready, b * QT + t + 1)
                                mm = pe.transpose(bank[:, j * P:(j + 1) * P], X[:, t, i * P:(i + 1) * P], ident[:])
                        elif kind == "qk":
                            if c == 0:
                                per = (2 if i % 4 < 2 else 1)
                                pe.wait_ge(wqk_in[i % 4], b * 32 * per + l * 16 * per + 16 * (i // 4 + 1))
                            if i == 0:
                                pe.wait_ge(proj_done, b * 2 * PROJ + l * PROJ + done("x", KT - 1, c))
                            w = wqk[:, i % 4, :].rearrange("p (h k c) -> p h k c", h=2, k=KT)
                            sl = slice(c * CH, (c + 1) * CH)
                            for k in range(KT):
                                mm = split_product(bank, w[:, 0, k, :], w[:, 1, k, :], xT[:, 0, k, sl], xT[:, 1, k, sl],
                                                   k == 0, k == KT - 1)
                        else:
                            if i == 0:
                                pe.wait_ge(wv_in, b * 32 + l * 16 + 16)
                            sl = slice(i * P, (i + 1) * P)
                            for k in range(KT):
                                mm = split_product(bank[:, 0:D], xT[:, 0, k, sl], xT[:, 1, k, sl], wv[:, 0, k, :], wv[:, 1, k, :],
                                                   k == 0, k == KT - 1)
                        mm.then_inc(proj_ready, 1)

                    n, G, vc = STEPS[l], GROUP[l], VCOL[l]
                    pe.wait_ge(proj_done, b * 2 * PROJ + (l + 1) * PROJ)
                    for i in range(-AHEAD, n + G + 2):
                        s = i + AHEAD
                        if s < n:
                            t, h = s // HEADS[l], s % HEADS[l]
                            if s >= 2:
                                pe.wait_ge(sum_ready, b * NSTEP + STEP0[l] + s - 1)
                            if t == 0 and (h == 0 or head_tile(l, h) > head_tile(l, h - 1)):
                                for q in range(2):
                                    wait_stacks(pe, b, l, head_tile(l, h), q)
                            q_s = stack(l, 0, h)[:, t * P:(t + 1) * P]
                            for c in range(NC):
                                dst, sl = ps[:, 2 * (s % 2) + c, :], slice(c * CH, (c + 1) * CH)
                                mm = pe.matmul(dst, q_s, stack(l, 1, h)[:, sl], start=True, stop=(l == 1))
                                if l == 0:
                                    mm = pe.matmul(dst, q_s[0:HD[0]], stack(l, 2, h)[0:HD[0], sl], start=False, stop=True)
                            mm.then_inc(scores_ready, 1)
                        if 0 <= i < n:
                            pe.wait_ge(exp_ready, b * NSTEP + STEP0[l] + i + 1)
                            for part, evac in ((0, pt_evacA), (1, pt_evacB)):
                                if i >= 1:
                                    pe.wait_ge(evac, b * NSTEP + STEP0[l] + i)
                                for k in range(4):
                                    kk = part * 4 + k
                                    mm = pe.transpose(ps[:, 4 + part, k * P:(k + 1) * P],
                                                      T[:, i % TS, kk * P:(kk + 1) * P], ident[:])
                                mm.then_inc(pt_ready, 1)
                        if i > G and last_of_group(l, i - G - 1):
                            g = (i - G - 1) // G
                            pe.wait_ge(ot_evac, b * NGROUP + GROUP0[l] + g + 1)
                            pe.transpose(ps[:, 6 + g % 2, 0:P], OT[:, g % 2, :], ident[:]).then_inc(ob_ready, 1)
                        if G <= i < n + G:
                            g, part = i // G - 1, i % G
                            if part == 0:
                                pe.wait_ge(pt_evacA, b * NSTEP + STEP0[l] + i)
                                pe.wait_ge(pt_evacB, b * NSTEP + STEP0[l] + i)
                                if g >= 2:
                                    pe.wait_ge(norm_done, b * NGROUP + GROUP0[l] + g - 1)
                            for k in range(part * QT // G, (part + 1) * QT // G):
                                for j in range(G):
                                    s2 = g * G + j
                                    mm = pe.matmul(ps[j * vc:j * vc + HD[l], 6 + g % 2, 0:P],
                                                   V[:, k, v_cols(l, s2 % HEADS[l])],
                                                   PT[:, pt_slot(s2), k, :], start=(k == 0), stop=(k == QT - 1))
                            if part == G - 1:
                                mm.then_inc(pv_ready, 1)

                    pe.wait_ge(norm_done, b * NGROUP + GROUP0[l] + GROUPS[l])
                    pe.wait_ge(pt_evacA, b * NSTEP + STEP0[l] + n)
                    pe.wait_ge(pt_evacB, b * NSTEP + STEP0[l] + n)
                    if l == 0:
                        for k in range(NC * KT):
                            transposed_unit(pe, k)
                        pe.wait_ge(wo_in, b * 16 + 16)
                        for t in range(QT):
                            c, j = t // TPC, t % TPC
                            if j == 0:
                                pe.wait_ge(tr_lo, b * TR + (c + 1) * KT)
                            sl = slice(j * P, (j + 1) * P)
                            for k in range(KT):
                                mm = split_product(ps[:, ao_bank(t), 0:D], xT1[:, c, 0, k, sl], xT1[:, c, 1, k, sl],
                                                   wos[:, 0, k, :], wos[:, 1, k, :], k == 0, k == KT - 1)
                            mm.then_inc(ao_ready, 1)
                            if t == QT - 2:
                                pe.wait_ge(x1_ready, b * QT + TPC)
                                for k in range(KT):
                                    transposed_unit(pe, NC * KT + k)

                        def hidden(k):
                            c, f = k // FT, k % FT
                            if f == 0:
                                pe.wait_ge(tr_lo, b * TR + NC * KT + (c + 1) * KT)
                            if c == 0:
                                pe.wait_ge(ff_in[f], b * 16 + 16)
                            if k >= 3:
                                pe.wait_ge(h_hi, b * HU + k - 2)
                            elif k < 2:
                                pe.wait_ge(res_ready, b * 2 * QT + QT - 1 + k)
                            w = arena[:, f * 2 * half:f * 2 * half + half].rearrange("p (h k c) -> p h k c", h=2, k=KT)
                            for kk in range(KT):
                                mm = split_product(ps[:, 4 + k % 3, :], w[:, 0, kk, :], w[:, 1, kk, :],
                                                   xT1[:, c, 0, kk, :], xT1[:, c, 1, kk, :], kk == 0, kk == KT - 1)
                            mm.then_inc(h_ready, 1)

                        def result(k):
                            c, f = k // FT, k % FT
                            pe.wait_ge(h_lo, b * HU + k + 1)
                            w = arena[:, f * 2 * half + half:(f + 1) * 2 * half].rearrange("p (h n) -> p h n", h=2)
                            for j in range(TPC):
                                if c > 0 and f == 0:
                                    pe.wait_ge(res_ready, b * 2 * QT + QT + (c - 1) * TPC + j + 1)
                                sl = slice(j * P, (j + 1) * P)
                                mm = split_product(ps[:, j, 0:D], hT[:, k % 2, 0, sl], hT[:, k % 2, 1, sl],
                                                   w[:, 0, :], w[:, 1, :], f == 0, f == FT - 1)
                            mm.then_inc(y_step, 1)

                        hidden(0)
                        hidden(1)
                        for k in range(HU):
                            result(k)
                            if k + 2 < HU:
                                hidden(k + 2)
                            if k < KT:
                                pe.wait_ge(x1_ready, b * QT + QT)
                                if k > 0:
                                    pe.wait_ge(tr_lo, b * TR + NC * KT + KT + k)
                                transposed_unit(pe, NC * KT + KT + k)

_L0 = ['wq', 'bq', 'wk', 'bk', 'wv', 'bv', 'wo', 'bo', 'w1', 'b1', 'w2', 'b2', 'alpha1', 'gamma1', 'alpha2', 'gamma2']
_L1 = ['Wq', 'bq', 'Wk', 'bk', 'Wv', 'bv', 'beta']
_INS = ['x', 'adj'] + ['L0_gnn_' + n for n in _L0] + ['L1_gnn_' + n for n in _L1]


def kernel(**inputs):
    import numpy as _np
    import concourse.bacc as _bacc
    from concourse import mybir as _mybir
    from concourse.bass_utils import run_bass_kernel_spmd as _run

    nc = _bacc.Bacc("TRN2", target_bir_lowering=False, num_devices=1)
    arrays, args = {}, []
    for name in _INS:
        a = _np.ascontiguousarray(inputs[name])
        if a.ndim == 0:
            a = a.reshape(1)
        arrays[f"in_{name}"] = a
        args.append(nc.dram_tensor(f"in_{name}", a.shape, _mybir.dt.from_np(a.dtype), kind="ExternalInput").ap())
    o = nc.dram_tensor("out_0", (B, N, D), _mybir.dt.float32, kind="ExternalOutput").ap()
    gnn_kernel(nc, *args, o)
    r = _run(nc, [arrays], core_ids=[0])
    return r.results[0]["out_0"]
```

```python
from contextlib import ExitStack

import concourse.bass as bass
from concourse import mybir

F32 = mybir.dt.float32
F32R = mybir.dt.float32r
ALU = mybir.AluOpType
ACT = mybir.ActivationFunctionType

P = 128
B, N, D = 8, 1024, 384
FF = 1536
QT = N // P
KT = D // P
CH = 512
NC = N // CH
TPC = CH // P
FT = FF // P
HEADS = (8, 12)
HD = (D // HEADS[0], D // HEADS[1])
GROUP = (2, 4)
VCOL = (64, 32)
RMS_EPS, LN_EPS = 1e-6, 1e-5
MASKED = -9e15
BIG = 3.0e38

STEPS = [QT * h for h in HEADS]
STEP0 = [0, STEPS[0]]
NSTEP = sum(STEPS)
GROUPS = [STEPS[l] // GROUP[l] for l in (0, 1)]
GROUP0 = [0, GROUPS[0]]
NGROUP = sum(GROUPS)
QK = 2 * KT
UNITS = ([("x", k, 0) for k in range(KT)] + [("qk", u, 0) for u in range(2)] + [("v", t, 0) for t in range(TPC - 1)]
         + [("x", k, 1) for k in range(KT)] + [("v", TPC - 1, 0)] + [("qk", u, 1) for u in range(2)]
         + [unit for j in range(QT - TPC) for unit in (("qk", 2 + j, 0), ("qk", 2 + j, 1), ("v", TPC + j, 1))])
PROJ = len(UNITS)
SPLIT = PROJ - QT
TR = 2 * NC * KT
HU = NC * FT
LAST = 4
YS = HU - LAST - 1
ROOTS = 4 * QT
AHEAD = 3
TS = AHEAD + 1
PV_PARTS = (1, 4)
PTS = 8
AS = 2
ADJ_USES = QT // AS
STAT_LAG, LN_LAG = 1, 3


def done(kind, i, c):
    return UNITS.index((kind, i, c)) + 1


def bank_of(l, n):
    return ((7, 4, 5, 6, 0, 1, 2, 3) if l == 1 else (2, 3, 0, 1, 4, 5, 6, 7))[n % 8]


def head_pieces(layer, m):
    hd, out, d = HD[layer], [], m * P
    while d < (m + 1) * P:
        n = min(hd - d % hd, (m + 1) * P - d)
        out.append((d - m * P, d // hd, d % hd, n))
        d += n
    return out


def head_tile(layer, h):
    return ((h + 1) * HD[layer] - 1) // P


def stack_copies(layer, is_k):
    if layer == 0:
        return [(0, 1, 0), (0, 1, 48), (1, 2, 0)] if is_k else [(0, 0, 0), (1, 0, 48)]
    return [(0, 1, 0), (0, 1, 32), (1, 1, 64)] if is_k else [(0, 0, 0), (1, 0, 32), (0, 0, 64)]


HELPED = (5, 12)


def stack_dmas(layer, m, is_k):
    out = []
    for row, h, off, n in head_pieces(layer, m):
        for part, blk, at in stack_copies(layer, is_k):
            queue = int((len(out) + 1) * HELPED[0] // HELPED[1] > len(out) * HELPED[0] // HELPED[1])
            out.append((row, n, part, blk, h, at + off, queue))
    return out


def stack_sem(layer, m, is_k):
    return 2 if (layer, m, is_k) == (1, KT - 1, 1) else is_k


def staged(layer, m, s, queue):
    tiles = [(l, i) for l in range(layer + 1) for i in range(KT if l < layer else m + 1)]
    return 16 * sum(d[-1] == queue for l, i in tiles for w in range(2) if stack_sem(l, i, w) == s
                    for d in stack_dmas(l, i, w))


def gnn_kernel(nc, x, adj, wq0, bq0, wk0, bk0, wv0, bv0, wo, bo, w1, b1, w2, b2, al1, ga1, al2, ga2,
               wq1, bq1, wk1, bk1, wv1, bv1, beta, out):
    with ExitStack() as ctx:
        def sb(name, shape, dt=F32, at=ctx):
            return at.enter_context(nc.sbuf_tensor(name, shape, dt))

        def sem(name):
            return ctx.enter_context(nc.semaphore(name))

        def dram(name, shape):
            return nc.dram_tensor(name, shape, F32, kind="Internal").ap()

        d_qk = dram("split_qk", [2, KT, 2, P, 2 * KT * P])
        d_v = dram("split_v", [2, P, 2 * KT * D])
        d_o = dram("split_o", [P, 2 * KT * D])
        d_ff = dram("split_ff", [FT, P, 2 * 2 * KT * P])

        X = sb("X", [P, QT, D])
        O = sb("O", [P, QT, D])
        V = sb("V", [P, QT, D])
        bvb = sb("bvb", [P, 2, D])
        rowsc = sb("rowsc", [P, 6, D])
        bo_b, b2_b, al1_b, ga1_b, al2_b, ga2_b = (rowsc[:, i, :] for i in range(6))
        small = sb("small", [P, 4 * KT + FT + 4])
        bqk = small[:, 0:4 * KT].rearrange("p (l w m) -> p l w m", l=2, w=2)
        b1c = small[:, 4 * KT:4 * KT + FT]
        betac, powc, epsr, epsl = (small[:, 4 * KT + FT + i:4 * KT + FT + i + 1] for i in range(4))
        ident = sb("ident", [P, P])
        nmax = sb("nmax", [P, QT, HEADS[1]])
        rsum = sb("rsum", [P, QT, HEADS[1]])
        OT = sb("OT", [P, 2, P])
        stat = sb("stat", [P, QT, 13])
        arena = sb("arena", [P, 24 * N], F32R)

        proj = ExitStack()
        stg = sb("stg", [P, 2, 2, N], F32R, proj)
        xT = sb("xT", [P, 2, KT, N], F32R, proj)
        wv = sb("wv", [P, 2, KT, D], F32R, proj)
        wqk = sb("wqk", [P, 4, 2 * KT * P], F32R, proj)
        proj.close()
        attn = ExitStack()
        PT = sb("PT", [P, PTS, QT, P], at=attn)
        T = sb("T", [P, TS, N], at=attn)
        sb("below_wqk", [P, P + P], at=attn)
        maskt = sb("maskt", [P, N], at=attn)
        A = sb("A", [P, AS, N], at=attn)
        attn.close()
        ffn = ExitStack()
        hT = sb("hT", [P, LAST, 2, CH], F32R, ffn)
        xT1 = sb("xT1", [P, NC, 2, KT, CH], F32R, ffn)
        sb("below_wos", [P, 2 * KT * D], at=ffn)
        wos = sb("wos", [P, 2, KT, D], F32R, ffn)
        ffn.close()
        hs = V[:, 0:KT, :].rearrange("p k n -> p (k n)")[:, 0:2 * CH].rearrange("p (i n) -> p i n", i=2)
        sq = V[:, KT, :]

        ps = ctx.enter_context(nc.psum_tensor("ps", [P, 8, CH], F32))

        def f32(ap):
            return ap.bitcast(F32)

        raw = [r_.rearrange("p k n -> p (k n)") for r_ in (V[:, 0:KT, :], V[:, KT:2 * KT, :], O[:, 0:KT, :])]

        consts_in = sem("consts_in")
        bias_in = sem("bias_in")
        ident_zero = sem("ident_zero")
        consts_ready = sem("consts_ready")
        pconst_ready = sem("pconst_ready")
        raw_in = [sem(f"raw_in{i}") for i in range(3)]
        w_scaled = sem("w_scaled")
        w_hi = sem("w_hi")
        w_lo = sem("w_lo")
        split_out = [sem(f"split_out{i}") for i in range(3)]
        x_in = [sem(f"x_in{t}") for t in range(QT)]
        wqk_in = [sem(f"wqk_in{i}") for i in range(4)]
        wv_in = sem("wv_in")
        proj_ready = sem("proj_ready")
        proj_hi = sem("proj_hi")
        proj_done = sem("proj_done")
        stacked = [[sem(f"stacked_{w}_{e}") for w in ("q", "k", "last")] for e in ("sync", "gpsimd")]
        adj_in = [sem(f"adj_in{i}") for i in range(AS)]
        mask_step = sem("mask_step")
        mask_ready = sem("mask_ready")
        scores_ready = sem("scores_ready")
        sum_ready = sem("sum_ready")
        exp_ready = sem("exp_ready")
        pt_ready = sem("pt_ready")
        pt_evacA = sem("pt_evacA")
        pt_evacB = sem("pt_evacB")
        pv_ready = sem("pv_ready")
        ot_evac = sem("ot_evac")
        ob_ready = sem("ob_ready")
        recip_ready = sem("recip_ready")
        norm_done = sem("norm_done")
        wo_in = sem("wo_in")
        ff_in = [sem(f"ff_in{f}") for f in range(FT)]
        tr_ready = sem("tr_ready")
        tr_hi = sem("tr_hi")
        tr_lo = sem("tr_lo")
        ao_ready = sem("ao_ready")
        pre1_ready = sem("pre1_ready")
        res_ready = sem("res_ready")
        sq_ready = sem("sq_ready")
        x1_ready = sem("x1_ready")
        dve_step = sem("dve_step")
        rms_ready = sem("rms_ready")
        stats_step = sem("stats_step")
        waits_passed = sem("waits_passed")
        var_ready = sem("var_ready")
        ln_ready = sem("ln_ready")
        root_step = sem("root_step")
        pool_step = sem("pool_step")
        pre2_ready = sem("pre2_ready")
        h_ready = sem("h_ready")
        silu_ready = sem("silu_ready")
        h_hi = sem("h_hi")
        h_lo = sem("h_lo")
        y_step = sem("y_step")
        y_rows = sem("y_rows")
        x_ready = sem("x_ready")
        x_free = sem("x_free")
        out_ready = sem("out_ready")
        out_done = [sem(f"out_done{t}") for t in range(QT)]

        def rows(w):
            return w.rearrange("(k p) n -> p k n", p=P)

        PIECES = []
        for l, (wq_, wk_, wv_) in enumerate(((wq0, wk0, wv0), (wq1, wk1, wv1))):
            PIECES.append((rows(wq_), float(HD[l]) ** -0.5, [d_qk[l, m, 0] for m in range(KT)], "cols"))
            PIECES.append((rows(wk_), None, [d_qk[l, m, 1] for m in range(KT)], "cols"))
            PIECES.append((rows(wv_), None, [d_v[l]], "rows"))
        PIECES.append((rows(wo), None, [d_o], "rows"))
        half = 2 * KT * P
        for i in range(FT // KT):
            fs = range(i * KT, (i + 1) * KT)
            PIECES.append((rows(w1)[:, :, i * D:(i + 1) * D], None, [d_ff[f][:, 0:half] for f in fs], "cols"))
            PIECES.append((rows(w2)[:, i * KT:(i + 1) * KT, :], None, [d_ff[f][:, half:2 * half] for f in fs], "tiles"))
        NP_ = len(PIECES)
        PW = 2 * KT * D

        def split_view(i, part):
            s = arena[:, (i % 3) * PW:(i % 3 + 1) * PW]
            kind = PIECES[i][3]
            if kind == "cols":
                return s.rearrange("p (m h k c) -> p h k m c", m=KT, h=2, k=KT)[:, part]
            if kind == "rows":
                return s.rearrange("p (h k n) -> p h k n", h=2, k=KT)[:, part]
            return s.rearrange("p (f h n) -> p h f n", f=KT, h=2)[:, part]

        def raw_view(i):
            v = raw[i % 3]
            if PIECES[i][3] == "cols":
                return v.rearrange("p (k m c) -> p k m c", k=KT, m=KT)
            return v.rearrange("p (k n) -> p k n", k=KT)

        def all_split(q):
            return 16 * sum(piece_outs(j) for j in range(q, NP_, 3))

        def piece_outs(i):
            return len(PIECES[i][2])

        def outs_before(i):
            return sum(piece_outs(j) for j in range(i % 3, i + 1, 3))

        def stack(layer, block, h):
            c = (block * HEADS[layer] + h) * N
            return arena[0:96, c:c + N]

        def v_cols(layer, h):
            return slice(h * HD[layer], (h + 1) * HD[layer])

        def last_of_group(layer, s):
            return s < STEPS[layer] and s % GROUP[layer] == GROUP[layer] - 1

        def wait_alone(eng, sem_, value):
            eng.wait_ge(sem_, value)
            eng.sem_inc(waits_passed, 1)

        def first_weights(sp, l):
            for u in range(4):
                sp.dma_start(f32(wqk[:, u, :]), d_qk[l, u // 2, u % 2]).then_inc(wqk_in[u], 16)
            sp.dma_start(f32(wv[:]).rearrange("p h k n -> p (h k n)"), d_v[l]).then_inc(wv_in, 16)

        def store_and_next(sp, b, t):
            sp.wait_ge(x_free, b * QT + t + 1)
            nb = (b + 1) % B
            sp.dma_start(X[:, t, :], x[nb, t * P:(t + 1) * P, :]).then_inc(x_in[t], 16)
            sp.wait_ge(out_ready, b * QT + t + 1)
            sp.dma_start(out[b, t * P:(t + 1) * P, :], O[:, t, :]).then_inc(out_done[t], 16)

        def copy_stacks(eng, b, l, u, mine):
            m, is_k = u // 2, u % 2
            wait_alone(eng, proj_done, b * 2 * PROJ + l * PROJ + done("qk", u, 1))
            for row, n, part, blk, h, at, queue in stack_dmas(l, m, is_k):
                if queue == mine:
                    dst = arena[at:at + n, (blk * HEADS[l] + h) * N:(blk * HEADS[l] + h + 1) * N]
                    eng.dma_start(f32(dst), f32(staging(l, u, part)[row:row + n, :])
                                  ).then_inc(stacked[queue][stack_sem(l, m, is_k)], 16)

        def wait_stacks(eng, b, l, m, is_k):
            for s in (is_k,) if stack_sem(l, m, is_k) == is_k else (is_k, 2):
                for queue in range(2):
                    eng.wait_ge(stacked[queue][s], b * staged(1, KT - 1, s, queue) + staged(l, m, s, queue))

        def o_space(i):
            return O[:].rearrange("p t n -> p (t n)")[:, i * N:(i + 1) * N]

        def staging(l, u, part):
            if (l, u) != (1, QK - 1):
                return stg[:, u % 2, part, :]
            return wqk[:, 2:4, :].rearrange("p i n -> p (i n)")[:, 0:N] if part else o_space(0).bitcast(F32R)

        def adj_rows(l, t):
            return o_space(1) if l == 1 and t == 0 else A[:, (t + 1) % AS, :]

        def pt_slot(i):
            return (i + PTS // 2) % PTS

        def acts_b(l, i):
            return l == 1 and (i % 4 == 1 or i % 12 == 7)

        def rms(link, b, idx, t, gain):
            nc.vector.wait_ge(rms_ready, b * 2 * QT + idx + 1)
            link(nc.vector.scalar_tensor_tensor(out=O[:, t, :], in0=O[:, t, :], scalar=stat[:, t, 2:3], in1=gain,
                                                op0=ALU.mult, op1=ALU.mult))

        def layer_stats(b, src, idx, t):
            nc.vector.bn_stats(stat[:, t, 4:10], src).then_inc(stats_step, 1)
            wait_alone(nc.vector, stats_step, b * 2 * QT + idx + 1)
            nc.vector.bn_aggr(stat[:, t, 10:12], stat[:, t, 4:10]).then_inc(var_ready, 1)

        def layer_norm(b, src, dst, idx, t):
            nc.vector.wait_ge(ln_ready, b * 2 * QT + idx + 1)
            return nc.vector.tensor_scalar(dst, src, stat[:, t, 10:11], stat[:, t, 12:13], ALU.subtract, ALU.mult)

        def inverse_root(pool, b, n, src, eps, dst):
            nc.gpsimd.tensor_tensor(src, src, eps, ALU.add).then_inc(root_step, 1)
            pool.wait_ge(root_step, b * ROOTS + n)
            return nc.gpsimd.tensor_tensor(dst, src, powc, ALU.pow)

        def lo_tr(dve, b, k):
            c, kt = k % (NC * KT) // KT, k % KT
            dve.wait_ge(tr_hi, b * TR + k + 1)
            dve.tensor_tensor(xT1[:, c, 1, kt, :], ps[:, tr_bank(k), :], f32(xT1[:, c, 0, kt, :]), ALU.subtract
                              ).then_inc(tr_lo, 1)

        def tail_sum(dve, b, t):
            dve.wait_ge(pre2_ready, b * QT + t + 1)
            dve.wait_ge(y_rows, b * QT + t + 1)
            dve.tensor_tensor(O[:, t, :], ps[:, t % TPC, 0:D], O[:, t, :], ALU.add).then_inc(res_ready, 1)

        def tail_norms(dve, b, link, t):
            rms(link, b, QT + t, t, al2_b)
            dve.wait_ge(pool_step, b * QT + t + 1)
            link(dve.tensor_tensor(O[:, t, :], O[:, t, :], X[:, t, :], ALU.add))
            layer_stats(b, O[:, t, :], t, t)

        def tail_end(dve, b, t):
            layer_norm(b, O[:, t, :], X[:, t, :], t, t).then_inc(x_ready, 1)

        def lo_unit(dve, b, l, n):
            kind, i, c = UNITS[n]
            src, sl = ps[:, bank_of(l, n), :], slice(c * CH, (c + 1) * CH)
            if kind == "v":
                dve.wait_ge(proj_ready, b * 2 * PROJ + l * PROJ + n + 1)
                dve.tensor_tensor(V[:, i, :], src[:, 0:D], bvb[:, l, :], ALU.add).then_inc(proj_done, 1)
                return
            splits = sum(kind_ != "v" for kind_, _, _ in UNITS[0:n + 1])
            dve.wait_ge(proj_hi, b * 2 * SPLIT + l * SPLIT + splits)
            if kind == "x":
                dve.tensor_tensor(xT[:, 1, i, sl], src, f32(xT[:, 0, i, sl]), ALU.subtract).then_inc(proj_done, 1)
            else:
                m, is_k = i // 2, i % 2
                dve.scalar_tensor_tensor(
                    out=staging(l, i, 1)[:, sl], in0=src, scalar=bqk[:, l % 2, is_k, m:m + 1],
                    in1=f32(staging(l, i, 0)[:, sl]), op0=ALU.add, op1=ALU.subtract).then_inc(proj_done, 1)

        def feed_forward(b, link):
            dve = nc.vector
            for k in range(KT, NC * KT):
                lo_tr(dve, b, k)

            def x1(t):
                rms(link, b, t, t, al1_b)
                dve.tensor_tensor(O[:, t, :], O[:, t, :], ga1_b, ALU.add).then_inc(x1_ready, 1)

            for t in range(QT):
                dve.wait_ge(pre1_ready, b * QT + t + 1)
                dve.wait_ge(ao_ready, b * QT + t + 1)
                dve.tensor_tensor(O[:, t, :], ps[:, ao_bank(t), 0:D], O[:, t, :], ALU.add).then_inc(res_ready, 1)
                if t >= 2:
                    x1(t - 2)
                if t == QT - 2:
                    for k in range(KT):
                        lo_tr(dve, b, NC * KT + k)
            for t in range(QT - 2, QT):
                x1(t)

            for k in range(HU):
                dve.wait_ge(silu_ready, b * HU + k + 1)
                dve.wait_ge(h_hi, b * HU + k + 1)
                dve.tensor_tensor(hT[:, k % LAST, 1, :], hs[:, k % 2, :], f32(hT[:, k % LAST, 0, :]), ALU.subtract
                                  ).then_inc(h_lo, 1)
                if 2 <= k < 2 + KT:
                    lo_tr(dve, b, NC * KT + KT + k - 2)
                if k == FT:
                    for t in range(TPC):
                        tail_sum(dve, b, t)
                if k >= FT + 2 and k - FT - 2 < TPC:
                    tail_norms(dve, b, link, k - FT - 2)
                if k >= FT + 6 and k - FT - 6 < TPC:
                    tail_end(dve, b, k - FT - 6)
            for n in range(KT):
                lo_unit(dve, b, 1, n)
            for t in range(TPC, QT + 1):
                if t < QT:
                    tail_sum(dve, b, t)
                if t > TPC:
                    tail_norms(dve, b, link, t - 1)
            for t in range(TPC, QT):
                tail_end(dve, b, t)

        def tr_bank(k):
            if k < NC * KT:
                return k
            return (7, 0, 1)[k % KT] if k < NC * KT + KT else 7

        def ao_bank(t):
            return (6 + t) % 8

        def out_stats(b, t):
            nc.vector.wait_ge(x_free, b * QT + t + 1)
            layer_stats(b, O[:, t, :], QT + t, t)

        def transposed_unit(pe, k):
            c, kt = k % (NC * KT) // KT, k % KT
            for j in range(TPC):
                mm = pe.transpose(ps[:, tr_bank(k), j * P:(j + 1) * P], O[:, c * TPC + j, kt * P:(kt + 1) * P], ident[:])
            mm.then_inc(tr_ready, 1)

        block = ctx.enter_context(nc.Block())

        @block.sync
        def _(sp):
            for t in range(QT):
                sp.dma_start(X[:, t, :], x[0, t * P:(t + 1) * P, :]).then_inc(x_in[t], 16)
            for i in range(NP_ + 2):
                if i < NP_:
                    if i >= 3:
                        sp.wait_ge(w_lo, i - 2)
                    sp.dma_start(raw[i % 3].rearrange("p (k n) -> p k n", k=KT), PIECES[i][0]).then_inc(raw_in[i % 3], 16)
                j = i - 2
                if j >= 0:
                    sp.wait_ge(w_lo, j + 1)
                    s = arena[:, (j % 3) * PW:(j % 3 + 1) * PW].rearrange("p (d n) -> p d n", d=piece_outs(j))
                    for d, dst in enumerate(PIECES[j][2]):
                        sp.dma_start(dst, f32(s[:, d, :])).then_inc(split_out[j % 3], 16)
                if j == NP_ - 4:
                    for q in range(3):
                        sp.wait_ge(split_out[q], 16 * piece_outs(q))
                    first_weights(sp, 0)
            for q in range(3):
                sp.wait_ge(split_out[q], all_split(q))

            with sp.Fori(0, B) as b:
                for l in (0, 1):
                    if l == 1:
                        sp.wait_ge(ao_ready, b * QT + QT)
                        first_weights(sp, l)
                        sp.wait_ge(x_ready, b * QT + QT)
                        sp.dma_start(adj_rows(l, 0), adj[b, 0:P, :]).then_inc(adj_in[0], 16)
                    for u in range(QK):
                        copy_stacks(sp, b, l, u, 0)
                        if u + 4 < QK:
                            sp.wait_ge(proj_ready, b * 2 * PROJ + l * PROJ + done("qk", u, 1))
                            sp.dma_start(f32(wqk[:, u, :]), d_qk[l, (u + 4) // 2, u % 2]).then_inc(wqk_in[u], 16)
                        if u == 3 and l == 0:
                            sp.dma_start(adj_rows(l, 0), adj[b, 0:P, :]).then_inc(adj_in[0], 16)
                    if l == 1:
                        wait_stacks(sp, b, l, KT - 1, 1)
                    for t in range(1, QT):
                        if t >= AS:
                            sp.wait_ge(sum_ready, b * NSTEP + STEP0[l] + (t - AS + 1) * HEADS[l])
                        sp.dma_start(adj_rows(l, t), adj[b, t * P:(t + 1) * P, :]).then_inc(adj_in[t % AS], 16)
                        if l == 1 and t >= 3:
                            store_and_next(sp, b, t - 3)
                    if l == 0:
                        sp.wait_ge(sum_ready, b * NSTEP + STEPS[0])
                        sp.dma_start(f32(wos[:]).rearrange("p h k n -> p (h k n)"), d_o).then_inc(wo_in, 16)
                        sp.wait_ge(scores_ready, b * NSTEP + STEPS[0])
                        for f in range(FT):
                            w = 2 * half
                            sp.dma_start(f32(arena[:, f * w:(f + 1) * w]), d_ff[f]).then_inc(ff_in[f], 16)
                    else:
                        store_and_next(sp, b, QT - 3)
                        sp.wait_ge(sum_ready, b * NSTEP + NSTEP)
                        wait_alone(sp, pt_ready, b * 2 * NSTEP + 2 * NSTEP)
                        first_weights(sp, 0)
                        for t in range(QT - 2, QT):
                            store_and_next(sp, b, t)
                        for t in range(QT):
                            wait_alone(sp, out_done[t], b * 16 + 16)
            for i in range(4):
                sp.wait_ge(wqk_in[i], 16 * (2 * B * (2 if i < 2 else 1) + 1))
            sp.wait_ge(wv_in, 16 * (2 * B + 1))
            for t in range(QT):
                sp.wait_ge(x_in[t], 16 * (B + 1))

        @block.gpsimd
        def _(pool):
            nc.gpsimd.memset(ident[:], 0.0).then_inc(ident_zero, 1)
            pool.wait_ge(ident_zero, 1)
            nc.gpsimd.affine_select(out=ident[:], in_=ident[:], compare_op=ALU.not_equal, fill=1.0, base=0,
                                    pattern=[[-1, P]], channel_multiplier=1).then_inc(consts_ready, 1)
            nc.gpsimd.memset(powc, -0.5).then_inc(pconst_ready, 1)
            nc.gpsimd.memset(epsr, RMS_EPS).then_inc(pconst_ready, 1)
            nc.gpsimd.memset(epsl, LN_EPS).then_inc(pconst_ready, 1)
            for i, r in enumerate((bo, b2, al1, ga1, al2, ga2)):
                pool.dma_start(rowsc[:, i, :], r.partition_broadcast(P)).then_inc(consts_in, 16)
            for i, r in enumerate((bv0, bv1)):
                pool.dma_start(bvb[:, i, :], r.partition_broadcast(P)).then_inc(consts_in, 16)
            for i, r in enumerate((bq0, bk0, bq1, bk1)):
                pool.dma_start(bqk[:, i // 2, i % 2, :], r.rearrange("(m p) -> p m", p=P),
                               allow_slow_non_contiguous=True).then_inc(bias_in, 16)
            pool.dma_start(b1c, b1.rearrange("(m p) -> p m", p=P), allow_slow_non_contiguous=True).then_inc(bias_in, 16)
            pool.dma_start(betac, beta.partition_broadcast(P)).then_inc(bias_in, 16)
            pool.wait_ge(consts_in, 16 * 8)
            pool.wait_ge(bias_in, 16 * 6)
            pool.wait_ge(pconst_ready, 3)

            for q in range(3):
                pool.wait_ge(split_out[q], all_split(q))

            with pool.Fori(0, B) as b:
                for u in range(QK):
                    copy_stacks(pool, b, 0, u, 1)

                def x_plus_bo(t):
                    pool.wait_ge(tr_ready, b * TR + (t // TPC + 1) * KT)
                    nc.gpsimd.tensor_tensor(O[:, t, :], X[:, t, :], bo_b, ALU.add).then_inc(pre1_ready, 1)

                for t in range(QT - 2):
                    x_plus_bo(t)
                for t in range(QT):
                    pool.wait_ge(sq_ready, b * 2 * QT + t + 1)
                    inverse_root(pool, b, t + 1, stat[:, t, 0:1], epsr, stat[:, t, 2:3]).then_inc(rms_ready, 1)
                    if t < 2:
                        x_plus_bo(QT - 2 + t)
                for t in range(QT):
                    nc.gpsimd.tensor_tensor(X[:, t, :], X[:, t, :], ga2_b, ALU.add).then_inc(pool_step, 1)
                for t in range(QT):
                    pool.wait_ge(tr_ready, b * TR + NC * KT + (t // TPC + 1) * KT)
                    nc.gpsimd.tensor_tensor(O[:, t, :], O[:, t, :], b2_b, ALU.add).then_inc(pre2_ready, 1)
                n = QT
                for c in range(NC):
                    for t in range(c * TPC, (c + 1) * TPC):
                        n += 1
                        pool.wait_ge(sq_ready, b * 2 * QT + QT + t + 1)
                        inverse_root(pool, b, n, stat[:, t, 0:1], epsr, stat[:, t, 2:3]).then_inc(rms_ready, 1)
                    for t in range(c * TPC, (c + 1) * TPC):
                        n += 1
                        pool.wait_ge(var_ready, b * 2 * QT + t + 1)
                        inverse_root(pool, b, n, stat[:, t, 11:12], epsl, stat[:, t, 12:13]).then_inc(ln_ready, 1)
                def mask(t):
                    rows_, m = adj_rows(1, t), maskt[:]
                    if t == 1:
                        pool.wait_ge(proj_ready, b * 2 * PROJ + PROJ + done("qk", QK - 1, 1))
                    pool.wait_ge(mask_ready, b * QT + t)
                    wait_alone(pool, adj_in[t % AS], b * 32 * ADJ_USES + 16 * (ADJ_USES + t // AS + 1))
                    nc.gpsimd.tensor_scalar(m, rows_, 0.0, MASKED, ALU.is_le, ALU.mult).then_inc(mask_step, 1)
                    wait_alone(pool, mask_step, b * 2 * (QT - 1) + 2 * t - 1)
                    nc.gpsimd.tensor_scalar(rows_, rows_, betac[:, 0:1], None, ALU.mult).then_inc(mask_step, 1)
                    pool.wait_ge(mask_step, b * 2 * (QT - 1) + 2 * t)
                    nc.gpsimd.tensor_tensor(rows_, rows_, m, ALU.add).then_inc(mask_ready, 1)

                for u in range(QK):
                    copy_stacks(pool, b, 1, u, 1)
                for t in range(1, QT + 2):
                    if t < QT:
                        mask(t)
                    if t >= 2:
                        pool.wait_ge(norm_done, b * NGROUP + GROUP0[1] + (t - 1) * (HEADS[1] // GROUP[1]))
                        nc.gpsimd.tensor_tensor(O[:, t - 2, :], O[:, t - 2, :], X[:, t - 2, :], ALU.add).then_inc(x_free, 1)
                        pool.wait_ge(var_ready, b * 2 * QT + QT + t - 1)
                        inverse_root(pool, b, 3 * QT + t - 1, stat[:, t - 2, 11:12], epsl,
                                     stat[:, t - 2, 12:13]).then_inc(ln_ready, 1)

        @block.scalar
        def _(act):
            act.wait_ge(bias_in, 16 * 6)
            for l in (0, 1):
                nc.scalar.mul(bqk[:, l, 0, :], bqk[:, l, 0, :], float(HD[l]) ** -0.5).then_inc(w_scaled, 1)
            scaled = 2
            for i in range(NP_):
                act.wait_ge(raw_in[i % 3], 16 * (i // 3 + 1))
                if PIECES[i][1] is not None:
                    nc.scalar.mul(raw[i % 3], raw[i % 3], PIECES[i][1]).then_inc(w_scaled, 1)
                    scaled += 1
                    act.wait_ge(w_scaled, scaled)
                if i >= 3:
                    act.wait_ge(split_out[i % 3], 16 * outs_before(i - 3))
                nc.scalar.copy(split_view(i, 0), raw_view(i)).then_inc(w_hi, 1)

            def hi_unit(b, l, n):
                kind, i, c = UNITS[n]
                if kind == "v":
                    return
                act.wait_ge(proj_ready, b * 2 * PROJ + l * PROJ + n + 1)
                src, sl = ps[:, bank_of(l, n), :], slice(c * CH, (c + 1) * CH)
                if kind == "x":
                    nc.scalar.copy(xT[:, 0, i, sl], src).then_inc(proj_hi, 1)
                else:
                    m, is_k = i // 2, i % 2
                    if c == 0 and m > 0 and (l, i) != (1, QK - 1):
                        wait_stacks(act, b, l, m - 1, is_k)
                    nc.scalar.activation(staging(l, i, 0)[:, sl], src, ACT.Identity,
                                         bias=bqk[:, l, is_k, m:m + 1]).then_inc(proj_hi, 1)

            for n in range(KT):
                hi_unit(0, 0, n)

            def hi_tr(b, k):
                act.wait_ge(tr_ready, b * TR + k + 1)
                nc.scalar.copy(xT1[:, k % (NC * KT) // KT, 0, k % KT, :], ps[:, tr_bank(k), :]).then_inc(tr_hi, 1)

            with act.Fori(0, B) as b:
                for l in (0, 1):
                    for n in range(KT, PROJ):
                        hi_unit(b, l, n)

                    n = STEPS[l]
                    for i in range(-2, n + GROUP[l] + 2):
                        if i > GROUP[l] and last_of_group(l, i - GROUP[l] - 1):
                            g = (i - GROUP[l] - 1) // GROUP[l]
                            act.wait_ge(pv_ready, b * NGROUP + GROUP0[l] + g + 1)
                            if g >= 2:
                                act.wait_ge(ob_ready, b * NGROUP + GROUP0[l] + g - 1)
                            nc.scalar.copy(OT[:, g % 2, :], ps[:, 6 + g % 2, 0:P]).then_inc(ot_evac, 1)
                        if i == n:
                            for k in range(KT):
                                if l == 0:
                                    hi_tr(b, k)
                                else:
                                    hi_unit(b, 2, k)
                        if 0 <= i < n:
                            act.wait_ge(pt_ready, b * 2 * NSTEP + 2 * (STEP0[l] + i) + 1)
                            if i >= PTS:
                                act.wait_ge(pv_ready, b * NGROUP + GROUP0[l] + (i - PTS) // GROUP[l] + 1)
                            if i == PTS // 2:
                                for q in range(2):
                                    wait_stacks(act, b, l, KT - 1, q)
                            nc.scalar.copy(PT[:, pt_slot(i), 0:4, :], ps[:, 4, :].rearrange("p (k q) -> p k q", k=4)
                                           ).then_inc(pt_evacA, 1)
                            if acts_b(l, i):
                                act.wait_ge(pt_ready, b * 2 * NSTEP + 2 * (STEP0[l] + i) + 2)
                                nc.scalar.copy(PT[:, pt_slot(i), 4:8, :], ps[:, 5, :].rearrange("p (k q) -> p k q", k=4)
                                               ).then_inc(pt_evacB, 1)
                        s = i + 2
                        if s < n:
                            t, h = s // HEADS[l], s % HEADS[l]
                            act.wait_ge(sum_ready, b * NSTEP + STEP0[l] + s + 1)
                            nc.scalar.activation(T[:, s % TS, :], T[:, s % TS, :], ACT.Exp, bias=nmax[:, t, h:h + 1],
                                                 scale=-1.0, accum_out=rsum[:, t, h:h + 1]).then_inc(exp_ready, 1)
                    if l == 0:
                        def square(idx, t):
                            act.wait_ge(res_ready, b * 2 * QT + idx + 1)
                            if idx >= 1:
                                act.wait_ge(sq_ready, b * 2 * QT + idx)
                            nc.scalar.activation(sq, O[:, t, :], ACT.Square, scale=float(D) ** -0.5,
                                                 accum_out=stat[:, t, 0:1]).then_inc(sq_ready, 1)

                        for k in range(KT, NC * KT):
                            hi_tr(b, k)
                        for t in range(QT):
                            if t == QT - 1:
                                for k in range(KT):
                                    hi_tr(b, NC * KT + k)
                            square(t, t)
                        for k in range(HU):
                            f = k % FT
                            bank = ps[:, 4 + k % 3, :]
                            act.wait_ge(h_ready, b * HU + k + 1)
                            if k >= 2:
                                act.wait_ge(h_lo, b * HU + k - 1)
                            nc.scalar.activation(hs[:, k % 2, :], bank, ACT.Silu, bias=b1c[:, f:f + 1]).then_inc(silu_ready, 1)
                            if k >= LAST:
                                if k - LAST == FT - 1:
                                    act.wait_ge(y_rows, b * QT + TPC)
                                else:
                                    act.wait_ge(y_step, b * YS + k - LAST + 1 - (k - LAST >= FT))
                            nc.scalar.activation(hT[:, k % LAST, 0, :], bank, ACT.Silu, bias=b1c[:, f:f + 1]).then_inc(h_hi, 1)
                            if 2 <= k < 2 + KT:
                                hi_tr(b, NC * KT + KT + k - 2)
                            if k >= FT + 1 and k - FT - 1 < TPC:
                                square(QT + k - FT - 1, k - FT - 1)
                        for n in range(KT):
                            hi_unit(b, 1, n)
                        for j in range(TPC):
                            square(QT + TPC + j, TPC + j)

        @block.vector
        def _(dve):
            dve.wait_ge(consts_in, 16 * 8)
            for i in range(NP_):
                dve.wait_ge(w_hi, i + 1)
                nc.vector.tensor_tensor(split_view(i, 1), raw_view(i), f32(split_view(i, 0)),
                                        ALU.subtract).then_inc(w_lo, 1)

            for n in range(KT):
                lo_unit(dve, 0, 0, n)
            LINKS = QT * 3 + 1
            with dve.Fori(0, B) as b:
                chain = [0]

                def link(ins):
                    chain[0] += 1
                    ins.then_inc(dve_step, 1)
                    dve.wait_ge(dve_step, b * LINKS + chain[0])

                for l in (0, 1):
                    for n in range(KT, PROJ):
                        lo_unit(dve, b, l, n)
                        if l == 1 and n == PROJ - QT:
                            dve.wait_ge(adj_in[0], b * 32 * ADJ_USES + 16 * (ADJ_USES + 1))
                            link(dve.tensor_scalar(o_space(2), adj_rows(1, 0), 0.0, MASKED, ALU.is_le, ALU.mult))
                            dve.scalar_tensor_tensor(out=adj_rows(1, 0), in0=adj_rows(1, 0), scalar=betac[:, 0:1],
                                                     in1=o_space(2), op0=ALU.mult, op1=ALU.add).then_inc(mask_ready, 1)

                    n = STEPS[l]
                    G, hd, vc = GROUP[l], HD[l], VCOL[l]
                    for i in range(-AHEAD, n + G + 2 + LN_LAG + 1):
                        s = i + AHEAD
                        if s < n:
                            t, h = s // HEADS[l], s % HEADS[l]
                            if h == 0:
                                if l == 1:
                                    dve.wait_ge(mask_ready, b * QT + t + 1)
                                else:
                                    dve.wait_ge(adj_in[t % AS], b * 32 * ADJ_USES + 16 * (t // AS + 1))
                            if s >= TS:
                                dve.wait_ge(pt_ready, b * 2 * NSTEP + 2 * (STEP0[l] + s - TS) + 2)
                            wait_alone(dve, scores_ready, b * NSTEP + STEP0[l] + s + 1)
                            nc.vector.tensor_tensor_reduce(
                                T[:, s % TS, :].rearrange("p (a n) -> p a n", a=2), ps[:, 2 * (s % 2):2 * (s % 2) + 2, :],
                                adj_rows(l, t).rearrange("p (a n) -> p a n", a=2), -1.0, BIG, ALU.add, ALU.min,
                                nmax[:, t, h:h + 1]).then_inc(sum_ready, 1)
                        if 0 <= i < n and not acts_b(l, i):
                            dve.wait_ge(pt_ready, b * 2 * NSTEP + 2 * (STEP0[l] + i) + 2)
                            if i >= PTS:
                                dve.wait_ge(pv_ready, b * NGROUP + GROUP0[l] + (i - PTS) // G + 1)
                            if i == PTS // 2:
                                for q in range(2):
                                    wait_stacks(dve, b, l, KT - 1, q)
                            nc.vector.tensor_copy(PT[:, pt_slot(i), 4:8, :], ps[:, 5, :].rearrange("p (k q) -> p k q", k=4)
                                                  ).then_inc(pt_evacB, 1)
                        if i == n:
                            for k in range(KT):
                                if l == 0:
                                    lo_tr(dve, b, k)
                                else:
                                    lo_unit(dve, b, 2, k)
                        if i >= 2 and last_of_group(l, i - 2):
                            g = (i - 2) // G
                            t, h0 = g * G // HEADS[l], g * G % HEADS[l]
                            dve.wait_ge(exp_ready, b * NSTEP + STEP0[l] + i - 1)
                            nc.vector.reciprocal(rsum[:, t, h0:h0 + G], rsum[:, t, h0:h0 + G]).then_inc(recip_ready, 1)
                        if i >= G + 2 and last_of_group(l, i - G - 2):
                            g = (i - G - 2) // G
                            t, h0 = g * G // HEADS[l], g * G % HEADS[l]
                            dve.wait_ge(recip_ready, b * NGROUP + GROUP0[l] + g + 1)
                            dve.wait_ge(ob_ready, b * NGROUP + GROUP0[l] + g + 1)
                            nc.vector.tensor_tensor(
                                O[:, t, h0 * hd:(h0 + G) * hd].rearrange("p (h d) -> p h d", h=G),
                                ps[:, 6 + g % 2, 0:P].rearrange("p (h d) -> p h d", h=G)[:, :, 0:hd],
                                rsum[:, t, h0:h0 + G].unsqueeze(2).to_broadcast([P, G, hd]),
                                ALU.mult).then_inc(norm_done, 1)
                        if l == 1:
                            for lag, part in ((STAT_LAG, out_stats), (LN_LAG, layer_norm)):
                                e = i - G - 2 - lag
                                if 0 <= e < n and e % HEADS[1] == HEADS[1] - 1:
                                    t = e // HEADS[1]
                                    if part is out_stats:
                                        out_stats(b, t)
                                    else:
                                        layer_norm(b, O[:, t, :], O[:, t, :], QT + t, t).then_inc(out_ready, 1)
                    if l == 0:
                        feed_forward(b, link)
                assert chain[0] == LINKS, chain[0]

        @block.tensor
        def _(pe):
            pe.wait_ge(consts_ready, 1)

            def split_product(dst, a_hi, a_lo, b_hi, b_lo, first, last):
                pe.matmul(dst, a_hi, b_hi, start=first, stop=False)
                pe.matmul(dst, a_hi, b_lo, start=False, stop=False)
                return pe.matmul(dst, a_lo, b_hi, start=False, stop=last)

            def project(b, l, n):
                kind, i, c = UNITS[n]
                at = bank_of(l, n)
                bank = ps[:, at, :]
                if n >= 8:
                    pe.wait_ge(proj_done, b * 2 * PROJ + l * PROJ + n - 7)
                elif l == 1:
                    if 1 <= n <= 3:
                        pe.wait_ge(h_hi, b * HU + HU - 3 + n)
                    elif at < 4:
                        pe.wait_ge(res_ready, b * 2 * QT + QT + TPC + at + 1)
                if kind == "x":
                    for j in range(TPC):
                        t = c * TPC + j
                        if i == 0:
                            if l != 1:
                                pe.wait_ge(x_in[t], b * 16 + 16 + l // 2 * 16)
                            else:
                                pe.wait_ge(x_ready, b * QT + t + 1)
                        mm = pe.transpose(bank[:, j * P:(j + 1) * P], X[:, t, i * P:(i + 1) * P], ident[:])
                elif kind == "qk":
                    if c == 0:
                        per = (2 if i % 4 < 2 else 1)
                        pe.wait_ge(wqk_in[i % 4], b * 32 * per + l * 16 * per + 16 * (i // 4 + 1))
                    if i == 0:
                        pe.wait_ge(proj_done, b * 2 * PROJ + l * PROJ + done("x", KT - 1, c))
                    w = wqk[:, i % 4, :].rearrange("p (h k c) -> p h k c", h=2, k=KT)
                    sl = slice(c * CH, (c + 1) * CH)
                    for k in range(KT):
                        mm = split_product(bank, w[:, 0, k, :], w[:, 1, k, :], xT[:, 0, k, sl], xT[:, 1, k, sl],
                                           k == 0, k == KT - 1)
                else:
                    if i == 0:
                        pe.wait_ge(wv_in, b * 32 + l * 16 + 16)
                    sl = slice(i * P, (i + 1) * P)
                    for k in range(KT):
                        mm = split_product(bank[:, 0:D], xT[:, 0, k, sl], xT[:, 1, k, sl], wv[:, 0, k, :], wv[:, 1, k, :],
                                           k == 0, k == KT - 1)
                mm.then_inc(proj_ready, 1)

            for n in range(KT):
                project(0, 0, n)

            with pe.Fori(0, B) as b:
                for l in (0, 1):
                    for n in range(KT, PROJ):
                        project(b, l, n)

                    n, G, vc = STEPS[l], GROUP[l], VCOL[l]
                    pe.wait_ge(proj_done, b * 2 * PROJ + (l + 1) * PROJ)
                    for i in range(-AHEAD, n + G + 2):
                        s = i + AHEAD
                        if s < n:
                            t, h = s // HEADS[l], s % HEADS[l]
                            if s >= 2:
                                pe.wait_ge(sum_ready, b * NSTEP + STEP0[l] + s - 1)
                            if t == 0 and (h == 0 or head_tile(l, h) > head_tile(l, h - 1)):
                                for q in range(2):
                                    wait_stacks(pe, b, l, head_tile(l, h), q)
                            q_s = stack(l, 0, h)[:, t * P:(t + 1) * P]
                            for c in range(NC):
                                dst, sl = ps[:, 2 * (s % 2) + c, :], slice(c * CH, (c + 1) * CH)
                                mm = pe.matmul(dst, q_s, stack(l, 1, h)[:, sl], start=True, stop=(l == 1))
                                if l == 0:
                                    mm = pe.matmul(dst, q_s[0:HD[0]], stack(l, 2, h)[0:HD[0], sl], start=False, stop=True)
                            mm.then_inc(scores_ready, 1)
                        if 0 <= i < n:
                            pe.wait_ge(exp_ready, b * NSTEP + STEP0[l] + i + 1)
                            for part, evac in ((0, pt_evacA), (1, pt_evacB)):
                                if i >= 1:
                                    pe.wait_ge(evac, b * NSTEP + STEP0[l] + i)
                                for k in range(4):
                                    kk = part * 4 + k
                                    mm = pe.transpose(ps[:, 4 + part, k * P:(k + 1) * P],
                                                      T[:, i % TS, kk * P:(kk + 1) * P], ident[:])
                                mm.then_inc(pt_ready, 1)
                        if i > G and last_of_group(l, i - G - 1):
                            g = (i - G - 1) // G
                            pe.wait_ge(ot_evac, b * NGROUP + GROUP0[l] + g + 1)
                            pe.transpose(ps[:, 6 + g % 2, 0:P], OT[:, g % 2, :], ident[:]).then_inc(ob_ready, 1)
                        if i == n:
                            pe.wait_ge(sum_ready, b * NSTEP + STEP0[l] + n)
                            if l == 0:
                                pe.wait_ge(norm_done, b * NGROUP + GROUPS[0] // NC)
                            for k in range(KT):
                                if l == 0:
                                    transposed_unit(pe, k)
                                else:
                                    project(b, 2, k)
                        every = G // PV_PARTS[l]
                        if G <= i < n + G and i % every == 0:
                            g, part = i // G - 1, i % G // every
                            if part == 0:
                                pe.wait_ge(pt_evacA, b * NSTEP + STEP0[l] + i)
                                pe.wait_ge(pt_evacB, b * NSTEP + STEP0[l] + i)
                                if g >= 2:
                                    pe.wait_ge(norm_done, b * NGROUP + GROUP0[l] + g - 1)
                            for k in range(part * QT // PV_PARTS[l], (part + 1) * QT // PV_PARTS[l]):
                                for j in range(G):
                                    s2 = g * G + j
                                    mm = pe.matmul(ps[j * vc:j * vc + HD[l], 6 + g % 2, 0:P],
                                                   V[:, k, v_cols(l, s2 % HEADS[l])],
                                                   PT[:, pt_slot(s2), k, :], start=(k == 0), stop=(k == QT - 1))
                            if part == PV_PARTS[l] - 1:
                                mm.then_inc(pv_ready, 1)

                    def last_banks_read():
                        pe.wait_ge(norm_done, b * NGROUP + GROUP0[l] + GROUPS[l])
                        pe.wait_ge(pt_evacA, b * NSTEP + STEP0[l] + n)
                        pe.wait_ge(pt_evacB, b * NSTEP + STEP0[l] + n)

                    if l == 1:
                        last_banks_read()
                    if l == 0:
                        pe.wait_ge(wo_in, b * 16 + 16)
                        pe.wait_ge(norm_done, b * NGROUP + GROUPS[0] - 1)
                        for t in range(QT):
                            c, j = t // TPC, t % TPC
                            if j == 0:
                                pe.wait_ge(tr_lo, b * TR + (c + 1) * KT)
                            sl = slice(j * P, (j + 1) * P)
                            for k in range(KT):
                                mm = split_product(ps[:, ao_bank(t), 0:D], xT1[:, c, 0, k, sl], xT1[:, c, 1, k, sl],
                                                   wos[:, 0, k, :], wos[:, 1, k, :], k == 0, k == KT - 1)
                            mm.then_inc(ao_ready, 1)
                            if t == 0:
                                last_banks_read()
                                for k in range(KT, NC * KT):
                                    transposed_unit(pe, k)
                            if t == QT - 2:
                                pe.wait_ge(x1_ready, b * QT + TPC)
                                for k in range(KT):
                                    transposed_unit(pe, NC * KT + k)

                        def hidden(k):
                            c, f = k // FT, k % FT
                            if f == 0:
                                pe.wait_ge(tr_lo, b * TR + NC * KT + (c + 1) * KT)
                            if c == 0:
                                pe.wait_ge(ff_in[f], b * 16 + 16)
                            if k >= 3:
                                pe.wait_ge(h_hi, b * HU + k - 2)
                            elif k < 2:
                                pe.wait_ge(res_ready, b * 2 * QT + QT - 1 + k)
                            w = arena[:, f * 2 * half:f * 2 * half + half].rearrange("p (h k c) -> p h k c", h=2, k=KT)
                            for kk in range(KT):
                                mm = split_product(ps[:, 4 + k % 3, :], w[:, 0, kk, :], w[:, 1, kk, :],
                                                   xT1[:, c, 0, kk, :], xT1[:, c, 1, kk, :], kk == 0, kk == KT - 1)
                            mm.then_inc(h_ready, 1)

                        def result(k, tiles):
                            c, f = k // FT, k % FT
                            w = arena[:, f * 2 * half + half:(f + 1) * 2 * half].rearrange("p (h n) -> p h n", h=2)
                            for j in tiles:
                                if c > 0 and f == 0:
                                    pe.wait_ge(res_ready, b * 2 * QT + QT + (c - 1) * TPC + j + 1)
                                sl = slice(j * P, (j + 1) * P)
                                mm = split_product(ps[:, j, 0:D], hT[:, k % LAST, 0, sl], hT[:, k % LAST, 1, sl],
                                                   w[:, 0, :], w[:, 1, :], f == 0, f == FT - 1)
                                if f == FT - 1:
                                    mm.then_inc(y_rows, 1)
                            return mm

                        hidden(0)
                        hidden(1)
                        for k in range(HU - LAST):
                            pe.wait_ge(h_lo, b * HU + k + 1)
                            mm = result(k, range(TPC))
                            if k != FT - 1:
                                mm.then_inc(y_step, 1)
                            hidden(k + 2)
                            if k < KT:
                                pe.wait_ge(x1_ready, b * QT + QT)
                                if k > 0:
                                    pe.wait_ge(tr_lo, b * TR + NC * KT + KT + k)
                                transposed_unit(pe, NC * KT + KT + k)
                        for k in range(HU - LAST + 2, HU):
                            hidden(k)
                        for n in range(KT):
                            project(b, 1, n)
                        pe.wait_ge(h_lo, b * HU + HU)
                        for j in range(TPC):
                            for k in range(HU - LAST, HU):
                                result(k, [j])

_L0 = ['wq', 'bq', 'wk', 'bk', 'wv', 'bv', 'wo', 'bo', 'w1', 'b1', 'w2', 'b2', 'alpha1', 'gamma1', 'alpha2', 'gamma2']
_L1 = ['Wq', 'bq', 'Wk', 'bk', 'Wv', 'bv', 'beta']
_INS = ['x', 'adj'] + ['L0_gnn_' + n for n in _L0] + ['L1_gnn_' + n for n in _L1]


def kernel(**inputs):
    import numpy as _np
    import concourse.bacc as _bacc
    from concourse import mybir as _mybir
    from concourse.bass_utils import run_bass_kernel_spmd as _run

    nc = _bacc.Bacc("TRN2", target_bir_lowering=False, num_devices=1)
    arrays, args = {}, []
    for name in _INS:
        a = _np.ascontiguousarray(inputs[name])
        if a.ndim == 0:
            a = a.reshape(1)
        arrays[f"in_{name}"] = a
        args.append(nc.dram_tensor(f"in_{name}", a.shape, _mybir.dt.from_np(a.dtype), kind="ExternalInput").ap())
    o = nc.dram_tensor("out_0", (B, N, D), _mybir.dt.float32, kind="ExternalOutput").ap()
    gnn_kernel(nc, *args, o)
    r = _run(nc, [arrays], core_ids=[0])
    return r.results[0]["out_0"]
```
